# Optimizing a Trainium2 kernel written in Bass

```python
import numpy as np
import jax
import jax.numpy as jnp

def _softmax(x, axis=-1):
    return jax.nn.softmax(x, axis=axis)

def _gelu(x):
    return jax.nn.gelu(x, approximate=True)

def _silu(x):
    return jax.nn.silu(x)

def _sigmoid(x):
    return jax.nn.sigmoid(x)

def _layernorm(x, axis=-1, eps=1e-05):
    m = jnp.mean(x, axis=axis, keepdims=True)
    v = jnp.var(x, axis=axis, keepdims=True)
    return (x - m) / jnp.sqrt(v + eps)

def _scatter_add(tgt, idx, src, axis=0):
    return tgt.at[idx].add(src)

def _segment_sum(src, seg, n):
    return jax.ops.segment_sum(src, seg, n)
kernel_name = 'mk_seq_preln_d1_jaxref_r4_24ad5a'

def setup_inputs(seed: int=0):
    np.random.seed(seed)
    _w = jnp.asarray

    def _L0_attn_setup():
        import jax, jax.numpy as jnp
        import numpy as np
        import math
        DIM = 256
        NUM_HEADS = 16
        HEAD_DIM = DIM // NUM_HEADS
        MAX_BIAS = 8.0
        SCALE = HEAD_DIM ** (-0.5)

        def _alibi_slopes(n):

            def pow2(n):
                start = 2.0 ** (-2.0 ** (-(math.log2(n) - 3)))
                return [start * start ** i for i in range(n)]
            if math.log2(n).is_integer():
                return pow2(n)
            c = 2 ** math.floor(math.log2(n))
            return pow2(c) + _alibi_slopes(2 * c)[0::2][:n - c]

        def _rotate_half(t):
            t1, t2 = jnp.split(t, 2, axis=-1)
            return jnp.concatenate([-t2, t1], axis=-1)
        key = jax.random.key(seed)
        k1, k2, k3, k4 = jax.random.split(key, 4)
        B, N, C = (2, 512, DIM)
        x = jax.random.normal(k1, (B, N, C), dtype=jnp.float32)
        qkv_w = jax.random.normal(k2, (3 * C, C), dtype=jnp.float32) * C ** (-0.5)
        proj_w = jax.random.normal(k3, (C, C), dtype=jnp.float32) * C ** (-0.5)
        proj_b = jax.random.normal(k4, (C,), dtype=jnp.float32) * 0.01
        slopes = jnp.asarray(np.array(_alibi_slopes(NUM_HEADS), dtype=np.float32))
        return {'x': x, 'qkv_w': qkv_w, 'proj_w': proj_w, 'proj_b': proj_b, 'slopes': slopes}
    _L0_attn_in = _L0_attn_setup()

    def _L0_ffn_setup():
        import jax, jax.numpy as jnp
        import numpy as np
        key = jax.random.key(seed)
        k1, k2, k3, k4, k5 = jax.random.split(key, 5)
        d_in, d_out, r = (256, 256, 32)
        x = jax.random.normal(k1, (8, 2048, d_in), dtype=jnp.float32)
        W = jax.random.normal(k2, (d_out, d_in), dtype=jnp.float32) * (1.0 / np.sqrt(d_in))
        b = jax.random.normal(k3, (d_out,), dtype=jnp.float32) * 0.01
        V_r = jax.random.normal(k4, (d_in, r), dtype=jnp.float32) * (1.0 / np.sqrt(d_in))
        C = jax.random.normal(k5, (d_out, r), dtype=jnp.float32) * (1.0 / np.sqrt(r))
        return {'x': x, 'W': W, 'b': b, 'V_r': V_r, 'C': C}
    _L0_ffn_in = _L0_ffn_setup()
    _d = {'L0_attn_x': _L0_attn_in['x'], 'L0_attn_qkv_w': _L0_attn_in['qkv_w'], 'L0_attn_proj_w': _L0_attn_in['proj_w'], 'L0_attn_proj_b': _L0_attn_in['proj_b'], 'L0_attn_slopes': _L0_attn_in['slopes'], 'L0_ffn_W': _L0_ffn_in['W'], 'L0_ffn_b': _L0_ffn_in['b'], 'L0_ffn_V_r': _L0_ffn_in['V_r'], 'L0_ffn_C': _L0_ffn_in['C']}
    _x0 = _d['L0_attn_x']
    _d['L0_attn_x'] = jax.random.normal(jax.random.fold_in(jax.random.key(seed), 1), (32, 512, 256), dtype=_x0.dtype)
    del _x0
    return _d

def reference(L0_attn_x, L0_attn_qkv_w, L0_attn_proj_w, L0_attn_proj_b, L0_attn_slopes, L0_ffn_W, L0_ffn_b, L0_ffn_V_r, L0_ffn_C):

    def _L0_attn_ref(x, qkv_w, proj_w, proj_b, slopes):
        import jax, jax.numpy as jnp
        import numpy as np
        import math
        DIM = 256
        NUM_HEADS = 16
        HEAD_DIM = DIM // NUM_HEADS
        MAX_BIAS = 8.0
        SCALE = HEAD_DIM ** (-0.5)

        def _alibi_slopes(n):

            def pow2(n):
                start = 2.0 ** (-2.0 ** (-(math.log2(n) - 3)))
                return [start * start ** i for i in range(n)]
            if math.log2(n).is_integer():
                return pow2(n)
            c = 2 ** math.floor(math.log2(n))
            return pow2(c) + _alibi_slopes(2 * c)[0::2][:n - c]

        def _rotate_half(t):
            t1, t2 = jnp.split(t, 2, axis=-1)
            return jnp.concatenate([-t2, t1], axis=-1)
        B, N, C = x.shape
        H, D = (NUM_HEADS, HEAD_DIM)
        qkv = (x @ qkv_w.T).reshape(B, N, 3, H, D).transpose(2, 0, 3, 1, 4)
        q, k, v = (qkv[0], qkv[1], qkv[2])
        inv_freq = 1.0 / 10000.0 ** (jnp.arange(0, D, 2, dtype=jnp.float32) / D)
        freqs = jnp.arange(N, dtype=jnp.float32)[:, None] * inv_freq[None, :]
        sin = jnp.tile(jnp.sin(freqs), (1, 2))
        cos = jnp.tile(jnp.cos(freqs), (1, 2))
        q = q * cos + _rotate_half(q) * sin
        k = k * cos + _rotate_half(k) * sin
        attn = jnp.einsum('bhqd,bhkd->bhqk', q, k) * SCALE
        pos = jnp.arange(N, dtype=jnp.float32)
        diff = pos[None, :] - pos[:, None]
        diff = jnp.where(diff > 0, 0.0, diff)
        alibi = diff[None, :, :] * slopes[:, None, None] * MAX_BIAS
        attn = attn + alibi[None]
        w = jax.nn.softmax(attn, axis=-1)
        out = jnp.einsum('bhqk,bhkd->bhqd', w, v)
        out = out.transpose(0, 2, 1, 3).reshape(B, N, C)
        return out @ proj_w.T + proj_b

    def _L0_ffn_ref(x, W, b, V_r, C):
        import jax, jax.numpy as jnp
        import numpy as np
        base = jnp.einsum('bsd,od->bso', x, W) + b
        correction = jnp.einsum('bsr,or->bso', jnp.einsum('bsd,dr->bsr', x, V_r), C)
        return base + correction
    x = L0_attn_x
    x = x + _L0_attn_ref(_layernorm(x, axis=-1), L0_attn_qkv_w, L0_attn_proj_w, L0_attn_proj_b, L0_attn_slopes)
    x = x + _L0_ffn_ref(_layernorm(x, axis=-1), L0_ffn_W, L0_ffn_b, L0_ffn_V_r, L0_ffn_C)
    return x

_drawn_inputs = setup_inputs


def setup_inputs(seed=0):
    import zlib

    import numpy as np

    out = dict(_drawn_inputs(seed))
    spreads = {}
    factors = {'L0_attn_proj_b': 6.307, 'L0_ffn_b': 8.0}
    for name, (base, spread) in spreads.items():
        noise = np.random.default_rng([zlib.crc32(name.encode()), seed]).standard_normal(out[name].shape)
        drawn = base * np.exp(spread * noise) if base else spread * noise
        out[name] = jnp.asarray(drawn.astype(out[name].dtype))
    for name, factor in factors.items():
        out[name] = (out[name] * factor).astype(out[name].dtype)
    return out
```

```python
from contextlib import ExitStack

import numpy as np
import concourse.bass as bass
from concourse import mybir

F32 = mybir.dt.float32
BF16 = mybir.dt.bfloat16
ALU = mybir.AluOpType
ACT = mybir.ActivationFunctionType

P = 128
NB, N, C = 32, 512, 256
H, D = 16, 16
T = N // P
KC = C // P
HG = 4
G = H // HG
R_LORA = 32
MAX_BIAS = 8.0
SCALE = float(D) ** -0.5
EPS = 1e-5
LOWEST = -3.0e38

QK_ROWS = 6 * D
M_ROW = QK_ROWS
BIAS_ROW = M_ROW + 2 * HG
U_W = N + (T - 1) * P

S_LOAD, S_STAT, S_NORM = -14, -12, -10
S_XT, S_G0, S_V = -8, -5, -5
S_U0 = -2
S_VCOPY0 = -2
S_MS0, S_E0, S_PV0, S_O0 = 5, 6, 7, 12
S_RES, S_RESB, S_F1, S_F2, S_LN2, S_F3, S_F4 = 20, 22, 26, 28, 29, 30, 33
SHIFT = -S_LOAD
SLOTS = H
DEPTH = 3


def shape_constants():
    f = np.float32
    inv_freq = (f(1.0) / np.power(f(10000.0), np.arange(0, D, 2, dtype=f) / f(D))).astype(f)
    freqs = (np.arange(N, dtype=f)[:, None] * inv_freq[None, :]).astype(f)
    sin, cos = np.sin(freqs.astype(np.float64)).astype(f), np.cos(freqs.astype(np.float64)).astype(f)

    def tile(a):
        return np.repeat(a.reshape(T, P, 1, -1), HG, axis=2).transpose(1, 0, 2, 3)

    rope_cos = tile(np.concatenate([cos, cos], 1)).reshape(P, -1)
    rope_sin = tile(np.concatenate([-sin, sin], 1)).reshape(P, -1)
    q = np.arange(P, dtype=f)[:, None]
    toep = np.minimum(np.arange(U_W, dtype=f)[None, :] - (U_W - N) - q, 0).astype(f)
    diag = np.minimum(q - np.arange(P, dtype=f)[None, :], 0).astype(f)
    rows = P - M_ROW
    kpat, qpat = np.zeros((rows, N), f), np.zeros((rows, N), f)
    kpick, qpick = np.zeros((rows, 4), f), np.zeros((rows, 4), f)
    tile_of, within = np.arange(N) // P, np.arange(N) % P
    kpat[0:2 * HG] = 1.0
    r = BIAS_ROW - M_ROW
    for j in range(T - 1):
        later, mine = (tile_of > j).astype(f), (tile_of == j).astype(f)
        for part in range(3):
            kpat[r], qpat[r] = mine, -later * (within + 1)
            kpick[r, part], qpick[r, 3] = 1, 1
            r += 1
        for part in range(3):
            kpat[r], qpat[r] = mine * (P - 1 - within), -later
            kpick[r, 3], qpick[r, part] = 1, 1
            r += 1
        if j < T - 2:
            for part in range(3):
                kpat[r], qpat[r] = mine, -later * P * (tile_of - j - 1)
                kpick[r, part], qpick[r, 3] = 1, 1
                r += 1
    assert r == rows
    mrow = np.zeros((rows, H), f)
    for h in range(H):
        mrow[2 * (h % HG):2 * (h % HG) + 2, h] = -1.0
    return {"rope_cos": rope_cos, "rope_sin": rope_sin, "toep": toep, "diag": diag,
            "pat": np.stack([qpat, kpat], 1).reshape(rows, -1), "pick": np.concatenate([qpick, kpick, mrow], 1),
            "ident": np.eye(P, dtype=f)}


class Batch:

    def __init__(self, i, d):
        self.i, self.d = i, d

    def before(self):
        return Batch(self.i, self.d + 1)

    def index(self):
        return self.i - self.d


class Event:

    def __init__(self, sem, per, step=1):
        self.sem, self.per, self.step = sem, per, step

    def mark(self, instruction):
        instruction.then_inc(self.sem, self.step)

    def wait(self, engine, b, k):
        rest = (k - b.d * self.per) * self.step
        if isinstance(b.i, int):
            value = b.i * self.per * self.step + rest
            if value > 0:
                engine.wait_ge(self.sem, value)
        else:
            engine.wait_ge(self.sem, b.i * (self.per * self.step) + rest)


class MiscBank:

    def __init__(self, full):
        self.full = full
        self.base, self.slope, self.n = 0, 0, 0
        self.emptied = None

    def fill(self, pe):
        if self.emptied:
            ev, b, k = self.emptied
            ev.wait(pe, b, k)

    def filled(self, matmul, ev, b, k):
        matmul.then_inc(self.full, 1)
        self.n += 1
        self.emptied = (ev, b, k)

    def wait_full(self, engine, i):
        engine.wait_ge(self.full, i * self.slope + (self.base + self.n) if self.slope else self.base + self.n)


def layer(nc, x, qkv_w, proj_w, proj_b, slopes, w, wb, v_r, c_r, consts, out):
    pe, dve, act, pool, sp = nc.tensor, nc.vector, nc.scalar, nc.gpsimd, nc.sync
    ctx = ExitStack()
    with ctx:
        def sb(name, shape, dt=F32):
            return ctx.enter_context(nc.sbuf_tensor(name, shape, dt))

        def ps(name, shape, dt=F32):
            return ctx.enter_context(nc.psum_tensor(name, shape, dt))

        def sem(name):
            return ctx.enter_context(nc.semaphore(name))

        def event(name, per, step=1):
            return Event(sem(name), per, step)

        ident = sb("ident", [P, P])
        ident_b = sb("ident_b", [P, P], BF16)
        rope_cos = sb("rope_cos", [P, T * HG * D])
        rope_sin = sb("rope_sin", [P, T * HG * D])
        diag = sb("diag", [P, P])
        alibi = sb("alibi", [P, H, U_W])
        slope8 = sb("slope8", [P, H])
        wqkv_t = sb("wqkv_t", [P, KC, 3 * C])
        proj_t = sb("proj_t", [P, KC, C])
        ffn_t = sb("ffn_t", [P, KC, C])
        proj_bias = sb("proj_bias", [P, C])
        ffn_bias = sb("ffn_bias", [P, C])
        minus_half = sb("minus_half", [P, T])
        eps = sb("eps", [P, T])
        ones = sb("ones", [P, 1])

        x_in = sb("x_in", [P, T, C])
        stats = sb("stats", [P, 2, T, 6])
        mean_var = sb("mean_var", [P, 2, T, 2])
        var_eps = sb("var_eps", [P, 2, T])
        rstd = sb("rstd", [P, 2, T])
        x_hat = sb("x_hat", [P, T, C])
        xt = sb("xt", [P, KC, N])
        rope_a = sb("rope_a", [P, 2, T * HG * D])
        rope_b = sb("rope_b", [P, 2, T * HG * D])
        rest1 = sb("rest1", [P, 2, T * HG * D])
        qka = sb("qka", [P, 2, 2, T, HG, 6, D], BF16)
        at = sb("at", [P, H, 2, N], BF16)
        v_stage = sb("v_stage", [P, T, C])
        v_one = sb("v_one", [P, T, H, 32])
        row_max = sb("row_max", [P, 2, T, HG])
        max2 = sb("max2", [P, T, HG, 2], BF16)
        junk = sb("junk", [P, T, N], BF16)
        pt = sb("pt", [P, 2, T, N])
        o_sb = sb("o_sb", [P, HG, P])
        r_den = sb("r_den", [P, HG, T])
        attn = sb("attn", [P, T, C])
        attn_t = sb("attn_t", [P, KC, N])
        x_res = sb("x_res", [P, T, C])
        x1 = sb("x1", [P, T, C])
        x_hat2 = sb("x_hat2", [P, T, C])
        x2t = sb("x2t", [P, KC, N])
        y = sb("y", [P, T, C])

        ps_s = ps("ps_s", [P, 2, N])
        ps_t = ps("ps_t", [P, 2, 2, N])
        ps_o = ps("ps_o", [P, HG, P])
        ps_m = ps("ps_m", [P, 512])
        ps_mb = ps_m[:, :].bitcast(BF16)

        s_ld = sem("s_ld")
        s_w = sem("s_w")
        wld = pt[:, 0, :, :].rearrange("p a b -> p (a b)")
        wq_nat = wld[:, 0:6 * C].rearrange("p (a c) -> p a c", a=6)
        wld2 = pt[:, 1, :, :].rearrange("p a b -> p (a b)")
        proj_nat = wld2[:, 0:512].rearrange("p (a c) -> p a c", a=2)
        w_nat = wld2[:, 512:1024].rearrange("p (a c) -> p a c", a=2)
        vr_nat = wld2[:, 1024:1088].rearrange("p (a c) -> p a c", a=2)
        cr_nat = wld2[:, 1088:1152].rearrange("p (a c) -> p a c", a=2)
        toep = y[:, :, :].rearrange("p a b -> p (a b)")
        pat = x1[M_ROW:P, :, :].rearrange("p a b -> p (a b)").rearrange("p (s n) -> p s n", s=2)
        pick = x_hat[M_ROW:P, 0, 0:8 + H]
        side = x_hat[M_ROW:P, 1, 0:2 * H].rearrange("p (s h) -> p s h", s=2)
        part = x_hat[M_ROW:P, 2, 0:5 * H].rearrange("p (s h) -> p s h", s=5)
        partb = junk[M_ROW:P, 0, 0:3 * H].rearrange("p (s h) -> p s h", s=3)
        vc_t = x_res[0:R_LORA, 0:2, :].rearrange("p a b -> p (a b)")

        loads = [
            (ident[:, :], consts["ident"]), (rope_cos[:, :], consts["rope_cos"]),
            (rope_sin[:, :], consts["rope_sin"]), (diag[:, :], consts["diag"]),
            (toep[:, 0:U_W], consts["toep"]), (pat, consts["pat"].rearrange("p (s n) -> p s n", s=2)),
            (pick, consts["pick"]),
            (wq_nat, qkv_w.rearrange("(a p) c -> p a c", p=P)),
            (proj_nat, proj_w.rearrange("(a p) c -> p a c", p=P)),
            (w_nat, w.rearrange("(a p) c -> p a c", p=P)),
            (vr_nat, v_r.rearrange("(a p) c -> p a c", p=P)),
            (cr_nat, c_r.rearrange("(a p) c -> p a c", p=P)),
            (slope8[:, :], slopes.partition_broadcast(P)),
            (proj_bias[:, :], proj_b.partition_broadcast(P)),
            (ffn_bias[:, :], wb.partition_broadcast(P)),
        ]
        for dst, src in loads:
            sp.dma_start(dst, src).then_inc(s_ld, 16)
        n_ld = 16 * len(loads)

        step = [0]

        def chain(engine, instruction):
            instruction.then_inc(s_w, 1)
            step[0] += 1

        def after_chain(engine):
            engine.wait_ge(s_w, step[0])

        dve.wait_ge(s_ld, n_ld)
        dve.memset(v_one[:, :, :, :], 1.0)
        dve.memset(ps_o[:, :, :], 0.0)
        dve.memset(minus_half[:, :], -0.5)
        dve.memset(eps[:, :], EPS)
        dve.memset(ones[:, :], 1.0)
        dve.tensor_copy(ident_b[:, :], ident[:, :])
        dve.tensor_scalar(wq_nat[:, 0:2, :], wq_nat[:, 0:2, :], SCALE, None, ALU.mult)
        chain(dve, dve.tensor_scalar(slope8[:, :], slope8[:, :], MAX_BIAS, None, ALU.mult))
        after_chain(dve)
        for h in range(H):
            ins = dve.tensor_scalar(alibi[:, h, :], toep[:, 0:U_W], slope8[:, h:h + 1], None, ALU.mult)
        chain(dve, ins)
        s8 = slope8[M_ROW:P, :]
        chain(dve, dve.tensor_copy(partb[:, 0, :], s8)); after_chain(dve)
        chain(dve, dve.tensor_tensor(part[:, 3, :], s8, partb[:, 0, :], ALU.subtract)); after_chain(dve)
        chain(dve, dve.tensor_copy(partb[:, 1, :], part[:, 3, :])); after_chain(dve)
        chain(dve, dve.tensor_tensor(part[:, 4, :], part[:, 3, :], partb[:, 1, :], ALU.subtract)); after_chain(dve)
        chain(dve, dve.tensor_copy(partb[:, 2, :], part[:, 4, :])); after_chain(dve)
        for s in range(2):
            chain(dve, dve.tensor_scalar(side[:, s, :], partb[:, 0, :], pick[:, 4 * s:4 * s + 1],
                                         pick[:, 4 * s + 3:4 * s + 4], ALU.mult, ALU.add)); after_chain(dve)
            for i in (1, 2):
                chain(dve, dve.scalar_tensor_tensor(out=side[:, s, :], in0=partb[:, i, :],
                                                    scalar=pick[:, 4 * s + i:4 * s + i + 1], in1=side[:, s, :],
                                                    op0=ALU.mult, op1=ALU.add)); after_chain(dve)
        chain(dve, dve.tensor_tensor(side[:, 1, :], side[:, 1, :], pick[:, 8:8 + H], ALU.add)); after_chain(dve)
        for h in range(H):
            for s in range(2):
                ins = dve.tensor_scalar(at[M_ROW:P, h, s, :], pat[:, s, :], side[:, s, h:h + 1], None, ALU.mult)
        chain(dve, ins)

        after_chain(pe)
        pe.wait_ge(s_ld, n_ld)
        flat_t = ps_t[:, :, :, :].rearrange("p u a n -> p (u a n)")
        for kc in range(KC):
            for a in range(6):
                pe.transpose(flat_t[:, kc * 1024 + a * P:kc * 1024 + (a + 1) * P],
                             wq_nat[:, a, kc * P:(kc + 1) * P], ident[:, :])
        for kc in range(KC):
            for a in range(2):
                pe.transpose(ps_s[:, kc, a * P:(a + 1) * P], proj_nat[:, a, kc * P:(kc + 1) * P], ident[:, :])
        for a in range(2):
            pe.transpose(ps_m[0:R_LORA, a * P:(a + 1) * P], vr_nat[:, a, :], ident[:, :])
        for a in range(2):
            ins = pe.transpose(ps_m[0:R_LORA, C + a * P:C + (a + 1) * P], cr_nat[:, a, :], ident[:, :])
        chain(pe, ins)
        after_chain(dve)
        for kc in range(KC):
            dve.tensor_copy(wqkv_t[:, kc, :], flat_t[:, kc * 1024:kc * 1024 + 3 * C])
            dve.tensor_copy(proj_t[:, kc, :], ps_s[:, kc, 0:C])
        chain(dve, dve.tensor_copy(vc_t, ps_m[0:R_LORA, :]))
        after_chain(pe)
        for kc in range(KC):
            for a in range(2):
                dst = ps_m[:, kc * C + a * P:kc * C + (a + 1) * P]
                pe.matmul(dst, vc_t[:, kc * P:(kc + 1) * P], vc_t[:, C + a * P:C + (a + 1) * P],
                          start=True, stop=False)
                ins = pe.matmul(dst, w_nat[:, a, kc * P:(kc + 1) * P], ident[:, :], start=False, stop=True)
        chain(pe, ins)
        after_chain(dve)
        chain(dve, dve.tensor_copy(ffn_t[:, :, :].rearrange("p a b -> p (a b)"), ps_m[:, :]))
        for engine in (pe, act, pool, sp, dve):
            after_chain(engine)

        e_load = event("e_load", 1, 16)
        e_aggr = event("e_aggr", 1)
        e_bn = event("e_bn", 1)
        e_veps = event("e_veps", 1)
        e_rstd = event("e_rstd", 1)
        e_xhat = event("e_xhat", 1)
        e_xt = event("e_xt", KC)
        e_rope = event("e_rope", G)
        e_qk = event("e_qk", G)
        e_hi = event("e_hi", G)
        e_r1 = event("e_r1", G)
        e_mid = event("e_mid", G)
        e_lo = event("e_lo", G)
        e_rep = event("e_rep", G)
        e_at = event("e_at", H)
        e_vs = event("e_vs", 2)
        e_v1 = event("e_v1", G)
        e_s = event("e_s", H * T)
        e_mx = event("e_mx", H * T)
        e_mhi = event("e_mhi", G)
        e_m2 = event("e_m2", G)
        e_mrow = event("e_mrow", G)
        e_st = event("e_st", H * 2)
        e_dg = event("e_dg", H * 2)
        e_ex = event("e_ex", H * 2)
        e_pv = event("e_pv", H)
        e_o = event("e_o", G)
        e_rden = event("e_rden", G)
        e_att = event("e_att", G)
        e_res = event("e_res", 1, 16)
        e_resb = event("e_resb", 1)
        e_aT = event("e_aT", KC)
        e_x1 = event("e_x1", 2)
        e_bn2 = event("e_bn2", 1)
        e_aggr2 = event("e_aggr2", 1)
        e_veps2 = event("e_veps2", 1)
        e_rstd2 = event("e_rstd2", 1)
        e_xhat2 = event("e_xhat2", 1)
        e_x1b = event("e_x1b", 1)
        e_x2t = event("e_x2t", KC)
        e_y = event("e_y", 2)
        e_out = event("e_out", 1, 16)
        misc = MiscBank(sem("misc_full"))

        def load_x(b):
            e_xhat.wait(sp, b.before(), 1)
            sp.dma_start(x_in[:, :, :], x[b.index()].rearrange("(t p) c -> p t c", p=P)) \
              .then_inc(e_load.sem, 16)

        def ln_stats(b, src, ln, bn, aggr, veps, rs):
            for t in range(T):
                ins = dve.bn_stats(stats[:, ln, t, :], src[:, t, :])
            bn.mark(ins)
            bn.wait(dve, b, 1)
            dve.nop(nofuse=True)
            for t in range(T):
                ins = dve.bn_aggr(mean_var[:, ln, t, :], stats[:, ln, t, :])
            aggr.mark(ins)
            aggr.wait(pool, b, 1)
            veps.mark(pool.tensor_tensor(var_eps[:, ln, :], mean_var[:, ln, :, 1], eps[:, :], ALU.add))
            veps.wait(pool, b, 1)
            rs.mark(pool.tensor_tensor(rstd[:, ln, :], var_eps[:, ln, :], minus_half[:, :], ALU.pow))

        def stats1(b):
            e_load.wait(dve, b, 1)
            ln_stats(b, x_in, 0, e_bn, e_aggr, e_veps, e_rstd)

        def normalise(b, src, dst, ln, rs, done):
            rs.wait(dve, b, 1)
            for t in range(T):
                ins = dve.tensor_scalar(dst[:, t, :], src[:, t, :], mean_var[:, ln, t, 0:1], rstd[:, ln, t:t + 1],
                                        ALU.subtract, ALU.mult)
            done.mark(ins)

        def transpose_tokens(b, kc, src, dst, ready, ready_n, done):
            misc.fill(pe)
            ready.wait(pe, b, ready_n)
            for t in range(T):
                ins = pe.transpose(ps_m[:, t * P:(t + 1) * P], src[:, t, kc * P:(kc + 1) * P], ident[:, :])
            misc.filled(ins, done, b, kc + 1)
            misc.wait_full(act, b.i)
            done.mark(act.copy(dst[:, kc, :], ps_m[:, :]))

        def project_qk(b, g):
            w0 = HG * D
            misc.fill(pe)
            if g == 0:
                e_xt.wait(pe, b, KC)
            for t in range(T):
                for kc in range(KC):
                    wt = wqkv_t[:, kc, 0:2 * C].rearrange("p (s o) -> p s o", s=2)[:, :, g * w0:(g + 1) * w0]
                    dst = ps_m[:, :].rearrange("p (s t o) -> p s t o", s=2, t=T)[:, :, t, :]
                    ins = pe.matmul(dst, xt[:, kc, t * P:(t + 1) * P], wt, start=(kc == 0), stop=(kc == KC - 1))
            misc.filled(ins, e_rope, b, g + 1)
            misc.wait_full(dve, b.i)
            prev = (b, g) if g else (b.before(), G)
            e_qk.wait(dve, *prev)
            m2 = ps_m[:, :].rearrange("p (s n) -> p s n", s=2)
            m4 = ps_m[:, :].rearrange("p (s n d) -> p s n d", s=2, d=D)
            b4 = rope_b[:, :, :].rearrange("p s (n d) -> p s n d", d=D)
            s4 = rope_sin[:, :].rearrange("p (o n d) -> p o n d", o=1, d=D)
            cos2 = rope_cos[:, :].rearrange("p (o n) -> p o n", o=1).broadcast_to([P, 2, T * HG * D])
            hd = D // 2
            dve.tensor_tensor(rope_a[:, :, :], m2, cos2, ALU.mult)
            for lo, hi in ((0, hd), (hd, 0)):
                ins = dve.tensor_tensor(b4[:, :, :, lo:lo + hd], m4[:, :, :, hi:hi + hd],
                                        s4[:, :, :, lo:lo + hd].broadcast_to([P, 2, T * HG, hd]), ALU.mult)
            e_rope.mark(ins)
            e_rope.wait(pool, b, g + 1)
            e_qk.mark(pool.tensor_tensor(rope_a[:, :, :], rope_a[:, :, :], rope_b[:, :, :], ALU.add))

        def split_qk(b, g):
            par = g % 2
            a3 = rope_a[:, :, :].rearrange("p s (n d) -> p (s n) d", d=D)
            r3 = rest1[:, :, :].rearrange("p s (n d) -> p (s n) d", d=D)
            q5 = qka[:, par, :, :, :, :, :].rearrange("p s t h e d -> p (s t h) e d")
            e_qk.wait(act, b, g + 1)
            e_hi.mark(act.copy(q5[:, :, 0, :], a3))
            e_hi.wait(pool, b, g + 1)
            e_r1.mark(pool.tensor_tensor(r3, a3, q5[:, :, 0, :], ALU.subtract))
            e_r1.wait(act, b, g + 1)
            e_mid.mark(act.copy(q5[:, :, 1, :], r3))
            e_mid.wait(pool, b, g + 1)
            n = T * HG
            pool.tensor_tensor(q5[:, 0:n, 5, :], r3[:, 0:n, :], q5[:, 0:n, 1, :], ALU.subtract)
            e_lo.mark(pool.tensor_tensor(q5[:, n:2 * n, 4, :], r3[:, n:2 * n, :], q5[:, n:2 * n, 1, :],
                                         ALU.subtract))

        def repeat_parts(b, g):
            par, n = g % 2, T * HG
            q5 = qka[:, par, :, :, :, :, :].rearrange("p s t h e d -> p (s t h) e d")
            e_mid.wait(dve, b, g + 1)
            dve.tensor_copy(q5[:, 0:n, 2:5:2, :], q5[:, 0:n, 0:1, :].broadcast_to([P, n, 2, D]))
            dve.tensor_copy(q5[:, n:2 * n, 3:6:2, :], q5[:, n:2 * n, 0:1, :].broadcast_to([P, n, 2, D]))
            dve.tensor_copy(q5[:, 0:n, 3, :], q5[:, 0:n, 1, :])
            e_rep.mark(dve.tensor_copy(q5[:, n:2 * n, 2, :], q5[:, n:2 * n, 1, :]))

        def operands(b, h):
            g, hh = divmod(h, HG)
            misc.fill(pe)
            if hh == 0:
                e_lo.wait(pe, b, g + 1)
                e_rep.wait(pe, b, g + 1)
            for s in range(2):
                for t in range(T):
                    ins = pe.transpose(ps_mb[0:QK_ROWS, s * N + t * P:s * N + (t + 1) * P],
                                       qka[:, g % 2, s, t, hh, :, :].rearrange("p e d -> p (e d)"), ident_b[:, :])
            misc.filled(ins, e_at, b, h + 1)
            misc.wait_full(act, b.i)
            e_at.mark(act.copy(at[0:QK_ROWS, h, :, :].rearrange("p s n -> p (s n)"), ps_mb[0:QK_ROWS, :]))

        def project_v(b, u):
            misc.fill(pe)
            if u == 0:
                e_xt.wait(pe, b, KC)
            for t in (2 * u, 2 * u + 1):
                for kc in range(KC):
                    ins = pe.matmul(ps_m[:, (t % 2) * C:(t % 2 + 1) * C], xt[:, kc, t * P:(t + 1) * P],
                                    wqkv_t[:, kc, 2 * C:3 * C], start=(kc == 0), stop=(kc == KC - 1))
            misc.filled(ins, e_vs, b, u + 1)
            misc.wait_full(act, b.i)
            e_v1.wait(act, b.before(), G)
            e_vs.mark(act.copy(v_stage[:, 2 * u:2 * u + 2, :].rearrange("p t c -> p (t c)"), ps_m[:, :]))

        def place_v(b, g):
            e_vs.wait(pool, b, 2)
            e_pv.wait(pool, b.before(), HG * (g + 1))
            one = ones[:, :].rearrange("p (a b c) -> p a b c", a=1, b=1).broadcast_to([P, T, HG, D])
            e_v1.mark(pool.tensor_tensor(
                v_one[:, :, g * HG:(g + 1) * HG, 0:D],
                v_stage[:, :, g * HG * D:(g + 1) * HG * D].rearrange("p t (h d) -> p t h d", d=D), one, ALU.mult))

        def max_scores(b, h, t):
            if t == 0:
                e_at.wait(pe, b, h + 1)
            k = h * T + t
            e_mx.wait(pe, b, k - 1)
            e_s.mark(pe.matmul(ps_s[:, t % 2, :], at[0:QK_ROWS, h, 0, t * P:(t + 1) * P],
                               at[0:QK_ROWS, h, 1, :], start=True, stop=True))

        def row_maximum(b, h, t):
            k = h * T + t
            g, hh = divmod(h, HG)
            if h % HG == 0 and t == 0:
                e_m2.wait(dve, *((b, g - 1) if g >= 2 else (b.before(), G + g - 1)))
            e_s.wait(dve, b, k + 1)
            dve.nop(nofuse=True)
            off = (T - 1 - t) * P
            e_mx.mark(dve.tensor_tensor_reduce(junk[:, t, :], ps_s[:, t % 2, :], alibi[:, h, off:off + N], 1.0, LOWEST,
                                               ALU.add, ALU.max, row_max[:, g % 2, t, hh:hh + 1]))

        def split_max(b, g):
            e_mx.wait(pool, b, (g + 1) * HG * T)
            e_mrow.wait(pool, *((b, g) if g else (b.before(), G)))
            one = ones[:, :].rearrange("p (a b) -> p a b", a=1).broadcast_to([P, T, HG])
            e_mhi.mark(pool.tensor_tensor(max2[:, :, :, 0], row_max[:, g % 2, :, :], one, ALU.mult))
            e_mhi.wait(pool, b, g + 1)
            e_m2.mark(pool.tensor_tensor(max2[:, :, :, 1], row_max[:, g % 2, :, :], max2[:, :, :, 0],
                                         ALU.subtract))

        def max_rows(b, g):
            misc.fill(pe)
            e_m2.wait(pe, b, g + 1)
            for t in range(T):
                ins = pe.transpose(ps_mb[M_ROW:BIAS_ROW, t * P:(t + 1) * P],
                                   max2[:, t, :, :].rearrange("p h e -> p (h e)"), ident_b[:, :])
            misc.filled(ins, e_mrow, b, g + 1)
            misc.wait_full(dve, b.i)
            src = ps_mb[M_ROW:BIAS_ROW, 0:N].rearrange("p (o n) -> p o n", o=1).broadcast_to([2 * HG, HG, N])
            e_mrow.mark(dve.tensor_copy(at[M_ROW:BIAS_ROW, g * HG:(g + 1) * HG, 0, :], src))

        def exp_scores(b, h, u):
            k = 2 * h + u
            if h % HG == 0 and u == 0:
                e_mrow.wait(pe, b, h // HG + 1)
            e_ex.wait(pe, b, k - 1)
            for jj in range(2):
                j = 2 * u + jj
                ins = pe.matmul(ps_t[:, u, jj, :], at[:, h, 1, j * P:(j + 1) * P], at[:, h, 0, :],
                                start=True, stop=True)
            e_st.mark(ins)

        def diagonal_bias(b, h, u):
            e_st.wait(dve, b, 2 * h + u + 1)
            first = ps_t[:, u, 0, 2 * u * P:(2 * u + 1) * P]
            blocks = bass.AP(first.tensor, first.offset, [first.ap[0], (N + P, 2), (1, P)])
            table = diag[:, :].rearrange("p (o q) -> p o q", o=1).broadcast_to([P, 2, P])
            e_dg.mark(dve.scalar_tensor_tensor(out=blocks, in0=table, scalar=slope8[:, h:h + 1], in1=blocks,
                                               op0=ALU.mult, op1=ALU.add))

        def exponentials(b, h, u):
            e_dg.wait(act, b, 2 * h + u + 1)
            if u == 0:
                e_pv.wait(act, b, h - 1)
            e_ex.mark(act.activation(pt[:, h % 2, 2 * u:2 * u + 2, :], ps_t[:, u, :, :], ACT.Exp))

        def weighted_values(b, h):
            e_ex.wait(pe, b, 2 * h + 2)
            g, hh = divmod(h, HG)
            if hh == 0:
                e_v1.wait(pe, b, g + 1)
                e_o.wait(pe, *((b, g) if g else (b.before(), G)))
            for j in range(T):
                for t in range(T):
                    ins = pe.matmul(ps_o[32 * t:32 * t + D + 1, hh, :], v_one[:, j, h, 0:D + 1],
                                    pt[:, h % 2, j, t * P:(t + 1) * P], start=(j == 0), stop=(j == T - 1),
                                    skip_group_check=True)
            e_pv.mark(ins)

        def o_out(b, g):
            e_pv.wait(act, b, HG * (g + 1))
            e_att.wait(act, *((b, g) if g else (b.before(), G)))
            e_o.mark(act.copy(o_sb[:, :, :], ps_o[:, :, :]))

        def attention_out(b, g):
            misc.fill(pe)
            e_o.wait(pe, b, g + 1)
            for hh in range(HG):
                ins = pe.transpose(ps_m[:, hh * P:(hh + 1) * P], o_sb[:, hh, :], ident[:, :])
            misc.filled(ins, e_att, b, g + 1)
            misc.wait_full(dve, b.i)
            o4 = ps_m[:, :].rearrange("p (h t d) -> p h t d", h=HG, t=T)
            e_rden.mark(dve.reciprocal(r_den[:, :, :], o4[:, :, :, D]))
            e_rden.wait(dve, b, g + 1)
            if g == 0:
                e_aT.wait(dve, b.before(), KC)
            dst = attn[:, :, g * HG * D:(g + 1) * HG * D].rearrange("p t (h d) -> p h t d", d=D)
            den = r_den[:, :, :].rearrange("p h (t o) -> p h t o", o=1).broadcast_to([P, HG, T, D])
            e_att.mark(dve.tensor_tensor(dst, o4[:, :, :, 0:D], den, ALU.mult))

        def load_residual(b):
            e_x1.wait(sp, b.before(), 2)
            sp.dma_start(x_res[:, :, :], x[b.index()].rearrange("(t p) c -> p t c", p=P)) \
              .then_inc(e_res.sem, 16)

        def residual_bias(b):
            e_res.wait(pool, b, 1)
            bias = proj_bias[:, :].rearrange("p (o c) -> p o c", o=1).broadcast_to([P, T, C])
            e_resb.mark(pool.tensor_tensor(x_res[:, :, :], x_res[:, :, :], bias, ALU.add))

        def out_projection(b, u):
            misc.fill(pe)
            if u == 0:
                e_aT.wait(pe, b, KC)
            for t in (2 * u, 2 * u + 1):
                for kc in range(KC):
                    ins = pe.matmul(ps_m[:, (t % 2) * C:(t % 2 + 1) * C], attn_t[:, kc, t * P:(t + 1) * P],
                                    proj_t[:, kc, :], start=(kc == 0), stop=(kc == KC - 1))
            misc.filled(ins, e_x1, b, u + 1)
            misc.wait_full(dve, b.i)
            if u == 0:
                e_resb.wait(dve, b, 1)
            two = slice(2 * u, 2 * u + 2)
            e_x1.mark(dve.tensor_tensor(x1[:, two, :], ps_m[:, :].rearrange("p (t c) -> p t c", t=2),
                                        x_res[:, two, :], ALU.add))

        def stats2(b):
            e_x1.wait(dve, b, 2)
            ln_stats(b, x1, 1, e_bn2, e_aggr2, e_veps2, e_rstd2)
            e_out.wait(pool, b.before(), 1)
            bias = ffn_bias[:, :].rearrange("p (o c) -> p o c", o=1).broadcast_to([P, T, C])
            e_x1b.mark(pool.tensor_tensor(y[:, :, :], x1[:, :, :], bias, ALU.add))

        def second_linear(b, u):
            misc.fill(pe)
            if u == 0:
                e_x2t.wait(pe, b, KC)
            for t in (2 * u, 2 * u + 1):
                for kc in range(KC):
                    ins = pe.matmul(ps_m[:, (t % 2) * C:(t % 2 + 1) * C], x2t[:, kc, t * P:(t + 1) * P],
                                    ffn_t[:, kc, :], start=(kc == 0), stop=(kc == KC - 1))
            misc.filled(ins, e_y, b, u + 1)
            misc.wait_full(dve, b.i)
            if u == 0:
                e_x1b.wait(dve, b, 1)
            two = slice(2 * u, 2 * u + 2)
            e_y.mark(dve.tensor_tensor(y[:, two, :], ps_m[:, :].rearrange("p (t c) -> p t c", t=2),
                                       y[:, two, :], ALU.add))

        def store(b):
            e_y.wait(sp, b, 2)
            sp.dma_start(out[b.index()].rearrange("(t p) c -> p t c", p=P), y[:, :, :]).then_inc(e_out.sem, 16)

        pieces = []

        def put(slot, order, piece, *args):
            pieces.append((slot + SHIFT, order, piece, args))

        put(S_LOAD, 0, load_x)
        put(S_STAT, 35, stats1)
        put(S_NORM, 35, lambda b: normalise(b, x_in, x_hat, 0, e_rstd, e_xhat))
        for kc in range(KC):
            put(S_XT + kc, 15, lambda b, kc=kc: transpose_tokens(b, kc, x_hat, xt, e_xhat, 1, e_xt))
        for g in range(G):
            put(S_G0 + HG * g, 45, project_qk, g)
            put(S_G0 + HG * g, 46, split_qk, g)
            put(S_G0 + HG * g + 1, 45, repeat_parts, g)
            put(S_VCOPY0 + HG * g, 50, place_v, g)
            put(S_MS0 + HG * g - 1, 48, split_max, g)
            put(S_MS0 + HG * g, 5, max_rows, g)
            put(S_O0 + HG * g - 1, 5, o_out, g)
            put(S_O0 + HG * g, 15, attention_out, g)
        for u in range(2):
            put(S_V, 15 + 10 * u, project_v, u)
            put(S_F2, 26 + 10 * u, out_projection, u)
            put(S_F4, 26 + 10 * u, second_linear, u)
        for h in range(H):
            put(S_U0 + h, 49, operands, h)
            put(S_PV0 + h, 47, weighted_values, h)
            for t in range(T):
                put(h, 10 + 10 * t, max_scores, h, t)
                put(h, 11 + 10 * t, row_maximum, h, t)
            for u in range(2):
                put(S_E0 + h, 22 + 20 * u, exp_scores, h, u)
                put(S_E0 + h, 23 + 20 * u, diagonal_bias, h, u)
                put(S_E0 + h, 24 + 20 * u, exponentials, h, u)
        for kc in range(KC):
            put(S_F1, 26 + 10 * kc, lambda b, kc=kc: transpose_tokens(b, kc, attn, attn_t, e_att, G, e_aT))
            put(S_F3, 26 + 10 * kc, lambda b, kc=kc: transpose_tokens(b, kc, x_hat2, x2t, e_xhat2, 1, e_x2t))
        put(S_RES, 0, load_residual)
        put(S_RESB, 50, residual_bias)
        put(S_LN2, 25, stats2)
        put(S_LN2, 48, lambda b: normalise(b, x1, x_hat2, 1, e_rstd2, e_xhat2))
        put(S_F4, 52, store)
        assert max(p[0] for p in pieces) < DEPTH * SLOTS
        pieces.sort(key=lambda p: (p[0] % SLOTS, p[1], p[0]))

        def body(i, alive):
            for slot, _, piece, args in pieces:
                d = slot // SLOTS
                if d in alive:
                    piece(Batch(i, d), *args)

        for i in range(DEPTH):
            body(i, [d for d in range(DEPTH) if 0 <= i - d < NB])

        units = sum(1 for p in pieces if p[2] in (project_qk, operands, project_v, max_rows, attention_out,
                                                  out_projection, second_linear)) + 3 * KC
        before = misc.n
        misc.fill(pe)
        ev, b, k = misc.emptied
        with nc.Fori(DEPTH, NB) as i:
            misc.slope, misc.base, misc.n = units, before - units * DEPTH, 0
            misc.emptied = (ev, Batch(i, b.d + 1), k)
            body(i, range(DEPTH))
            assert misc.n == units
            last = misc.emptied
        assert last[0] is ev and last[1].d == b.d and last[2] == k
        misc.slope, misc.base, misc.n = 0, 0, before + units * (NB - DEPTH)
        misc.emptied = (ev, Batch(NB - 1, b.d), k)
        for i in range(NB, NB + DEPTH - 1):
            body(i, [d for d in range(DEPTH) if 0 <= i - d < NB])
        e_out.wait(sp, Batch(NB - 1, 0), 1)


_INS = ["L0_attn_x", "L0_attn_qkv_w", "L0_attn_proj_w", "L0_attn_proj_b", "L0_attn_slopes",
        "L0_ffn_W", "L0_ffn_b", "L0_ffn_V_r", "L0_ffn_C"]


def kernel(**inputs):
    import numpy as _np
    import concourse.bacc as _bacc
    from concourse import mybir as _mybir
    from concourse.bass_utils import run_bass_kernel_spmd as _run

    nc = _bacc.Bacc("TRN2", target_bir_lowering=False, num_devices=1)
    arrays, args, consts = {}, [], {}
    for name in _INS:
        a = _np.ascontiguousarray(inputs[name])
        arrays[f"in_{name}_dram"] = a
        args.append(nc.dram_tensor(f"in_{name}_dram", a.shape, _mybir.dt.from_np(a.dtype),
                                   kind="ExternalInput").ap())
    for name, a in shape_constants().items():
        a = _np.ascontiguousarray(a)
        arrays[f"const_{name}_dram"] = a
        consts[name] = nc.dram_tensor(f"const_{name}_dram", a.shape, _mybir.dt.from_np(a.dtype),
                                      kind="ExternalInput").ap()
    out = nc.dram_tensor("out_dram", (NB, N, C), _mybir.dt.float32, kind="ExternalOutput").ap()
    layer(nc, *args, consts, out)
    r = _run(nc, [arrays], core_ids=[0])
    return r.results[0]["out_dram"]
```

```python
from contextlib import ExitStack

import numpy as np
import concourse.bass as bass
from concourse import mybir

F32 = mybir.dt.float32
BF16 = mybir.dt.bfloat16
ALU = mybir.AluOpType
ACT = mybir.ActivationFunctionType

P = 128
NB, N, C = 32, 512, 256
H, D = 16, 16
T = N // P
KC = C // P
HG = 4
G = H // HG
R_LORA = 32
MAX_BIAS = 8.0
SCALE = float(D) ** -0.5
EPS = 1e-5
LOWEST = -3.0e38

QK_ROWS = 6 * D
M_ROW = QK_ROWS
BIAS_ROW = M_ROW + 2 * HG
U_W = N + (T - 1) * P

S_LOAD, S_STAT, S_NORM = -12, -11, -10
S_XT, S_G0, S_V = -8, -5, -6
S_U0 = -2
S_VCOPY0 = -2
S_MS0, S_E0, S_PV0, S_O0 = 5, 7, 8, 13
S_RES, S_RESB, S_F1, S_F2, S_LN2, S_F3, S_F4 = 20, 22, 26, 29, 31, 32, 33
SHIFT = -S_LOAD
SLOTS = H
T_BANKS = 3
DEPTH = 3


def shape_constants():
    f = np.float32
    inv_freq = (f(1.0) / np.power(f(10000.0), np.arange(0, D, 2, dtype=f) / f(D))).astype(f)
    freqs = (np.arange(N, dtype=f)[:, None] * inv_freq[None, :]).astype(f)
    sin, cos = np.sin(freqs.astype(np.float64)).astype(f), np.cos(freqs.astype(np.float64)).astype(f)

    def tile(a):
        return np.repeat(a.reshape(T, P, 1, -1), HG, axis=2).transpose(1, 0, 2, 3)

    rope_cos = tile(np.concatenate([cos, cos], 1)).reshape(P, -1)
    rope_sin = tile(np.concatenate([-sin, sin], 1)).reshape(P, -1)
    q = np.arange(P, dtype=f)[:, None]
    toep = np.minimum(np.arange(U_W, dtype=f)[None, :] - (U_W - N) - q, 0).astype(f)
    diag = np.minimum(q - np.arange(P, dtype=f)[None, :], 0).astype(f)
    rows = P - M_ROW
    kpat, qpat = np.zeros((rows, N), f), np.zeros((rows, N), f)
    kpick, qpick = np.zeros((rows, 4), f), np.zeros((rows, 4), f)
    tile_of, within = np.arange(N) // P, np.arange(N) % P
    kpat[0:2 * HG] = 1.0
    r = BIAS_ROW - M_ROW
    for j in range(T - 1):
        later, mine = (tile_of > j).astype(f), (tile_of == j).astype(f)
        for part in range(3):
            kpat[r], qpat[r] = mine, -later * (within + 1)
            kpick[r, part], qpick[r, 3] = 1, 1
            r += 1
        for part in range(3):
            kpat[r], qpat[r] = mine * (P - 1 - within), -later
            kpick[r, 3], qpick[r, part] = 1, 1
            r += 1
        if j < T - 2:
            for part in range(3):
                kpat[r], qpat[r] = mine, -later * P * (tile_of - j - 1)
                kpick[r, part], qpick[r, 3] = 1, 1
                r += 1
    assert r == rows
    mrow = np.zeros((rows, H), f)
    for h in range(H):
        mrow[2 * (h % HG):2 * (h % HG) + 2, h] = -1.0
    return {"rope_cos": rope_cos, "rope_sin": rope_sin, "toep": toep, "diag": diag,
            "pat": np.stack([qpat, kpat], 1).reshape(rows, -1), "pick": np.concatenate([qpick, kpick, mrow], 1),
            "ident": np.eye(P, dtype=f)}


class Batch:

    def __init__(self, i, d):
        self.i, self.d = i, d

    def before(self):
        return Batch(self.i, self.d + 1)

    def index(self):
        return self.i - self.d


class Event:

    def __init__(self, sem, per, step=1):
        self.sem, self.per, self.step = sem, per, step

    def mark(self, instruction):
        instruction.then_inc(self.sem, self.step)

    def wait(self, engine, b, k):
        rest = (k - b.d * self.per) * self.step
        if isinstance(b.i, int):
            value = b.i * self.per * self.step + rest
            if value > 0:
                engine.wait_ge(self.sem, value)
        else:
            engine.wait_ge(self.sem, b.i * (self.per * self.step) + rest)


class MiscBanks:

    BANKS = 2

    def __init__(self, full):
        self.full = full
        self.base, self.slope, self.n = 0, 0, 0
        self.first = 0
        self.emptied = []

    def fill(self, pe):
        if len(self.emptied) == self.BANKS:
            ev, b, k = self.emptied[0]
            ev.wait(pe, b, k)
        return (self.first + self.n) % self.BANKS

    def filled(self, matmul, ev, b, k):
        matmul.then_inc(self.full, 1)
        self.n += 1
        self.emptied = self.emptied[-(self.BANKS - 1):] + [(ev, b, k)]
        return self.n

    def wait_full(self, engine, b, unit):
        engine.wait_ge(self.full, b.i * self.slope + (self.base + unit) if self.slope else self.base + unit)


def layer(nc, x, qkv_w, proj_w, proj_b, slopes, w, wb, v_r, c_r, consts, out):
    pe, dve, act, pool, sp = nc.tensor, nc.vector, nc.scalar, nc.gpsimd, nc.sync
    ctx = ExitStack()
    with ctx:
        def sb(name, shape, dt=F32):
            return ctx.enter_context(nc.sbuf_tensor(name, shape, dt))

        def ps(name, shape, dt=F32):
            return ctx.enter_context(nc.psum_tensor(name, shape, dt))

        def sem(name):
            return ctx.enter_context(nc.semaphore(name))

        def event(name, per, step=1):
            return Event(sem(name), per, step)

        ident = sb("ident", [P, P])
        ident_b = sb("ident_b", [P, P], BF16)
        rope_cos = sb("rope_cos", [P, T * HG * D])
        rope_sin = sb("rope_sin", [P, T * HG * D])
        diag = sb("diag", [P, P])
        alibi = sb("alibi", [P, H, U_W])
        slope8 = sb("slope8", [P, H])
        wqkv_t = sb("wqkv_t", [P, KC, 3 * C])
        proj_t = sb("proj_t", [P, KC, C])
        ffn_t = sb("ffn_t", [P, KC, C])
        proj_bias = sb("proj_bias", [P, C])
        ffn_bias = sb("ffn_bias", [P, C])
        minus_half = sb("minus_half", [P, T])
        eps = sb("eps", [P, T])
        ones = sb("ones", [P, 1])

        x_in = sb("x_in", [P, T, C])
        stats = sb("stats", [P, 2, T, 6])
        mean_var = sb("mean_var", [P, 2, T, 2])
        var_eps = sb("var_eps", [P, 2, T])
        rstd = sb("rstd", [P, 2, T])
        x_hat = sb("x_hat", [P, T, C])
        xt = sb("xt", [P, KC, N])
        rope_a = sb("rope_a", [P, 2, T * HG * D])
        rope_b = sb("rope_b", [P, 2, T * HG * D])
        rest1 = sb("rest1", [P, 2, T * HG * D])
        qka = sb("qka", [P, 2, 2, T, HG, 6, D], BF16)
        at = sb("at", [P, H, 2, N], BF16)
        v_stage = sb("v_stage", [P, T, C])
        v_one = sb("v_one", [P, T, H, 32])
        row_max = sb("row_max", [P, 2, T, HG])
        max2 = sb("max2", [P, T, HG, 2], BF16)
        max_t = sb("max_t", [P, N], BF16)
        junk = sb("junk", [P, T, N], BF16)
        pt = sb("pt", [P, 2, T, N])
        o_sb = sb("o_sb", [P, HG, P])
        r_den = sb("r_den", [P, HG, T])
        attn = sb("attn", [P, T, C])
        attn_t = sb("attn_t", [P, KC, N])
        x_res = sb("x_res", [P, T, C])
        x1 = sb("x1", [P, T, C])
        x_hat2 = sb("x_hat2", [P, T, C])
        x2t = sb("x2t", [P, KC, N])
        y = sb("y", [P, T, C])

        ps_s = ps("ps_s", [P, 2, N])
        ps_t = ps("ps_t", [P, T_BANKS, N])
        ps_o = ps("ps_o", [P, HG, P])
        ps_misc = ps("ps_misc", [P, MiscBanks.BANKS, 512])

        s_ld = sem("s_ld")
        s_w = sem("s_w")
        wld = pt[:, 0, :, :].rearrange("p a b -> p (a b)")
        wq_nat = wld[:, 0:6 * C].rearrange("p (a c) -> p a c", a=6)
        wld2 = pt[:, 1, :, :].rearrange("p a b -> p (a b)")
        proj_nat = wld2[:, 0:512].rearrange("p (a c) -> p a c", a=2)
        w_nat = wld2[:, 512:1024].rearrange("p (a c) -> p a c", a=2)
        vr_nat = wld2[:, 1024:1088].rearrange("p (a c) -> p a c", a=2)
        cr_nat = wld2[:, 1088:1152].rearrange("p (a c) -> p a c", a=2)
        toep = y[:, :, :].rearrange("p a b -> p (a b)")
        pat = x1[M_ROW:P, :, :].rearrange("p a b -> p (a b)").rearrange("p (s n) -> p s n", s=2)
        pick = x_hat[M_ROW:P, 0, 0:8 + H]
        side = x_hat[M_ROW:P, 1, 0:2 * H].rearrange("p (s h) -> p s h", s=2)
        part = x_hat[M_ROW:P, 2, 0:5 * H].rearrange("p (s h) -> p s h", s=5)
        partb = junk[M_ROW:P, 0, 0:3 * H].rearrange("p (s h) -> p s h", s=3)
        vc_t = x_res[0:R_LORA, 0:2, :].rearrange("p a b -> p (a b)")

        loads = [
            (ident[:, :], consts["ident"]), (rope_cos[:, :], consts["rope_cos"]),
            (rope_sin[:, :], consts["rope_sin"]), (diag[:, :], consts["diag"]),
            (toep[:, 0:U_W], consts["toep"]), (pat, consts["pat"].rearrange("p (s n) -> p s n", s=2)),
            (pick, consts["pick"]),
            (wq_nat, qkv_w.rearrange("(a p) c -> p a c", p=P)),
            (proj_nat, proj_w.rearrange("(a p) c -> p a c", p=P)),
            (w_nat, w.rearrange("(a p) c -> p a c", p=P)),
            (vr_nat, v_r.rearrange("(a p) c -> p a c", p=P)),
            (cr_nat, c_r.rearrange("(a p) c -> p a c", p=P)),
            (slope8[:, :], slopes.partition_broadcast(P)),
            (proj_bias[:, :], proj_b.partition_broadcast(P)),
            (ffn_bias[:, :], wb.partition_broadcast(P)),
        ]
        for dst, src in loads:
            sp.dma_start(dst, src).then_inc(s_ld, 16)
        n_ld = 16 * len(loads)

        step = [0]

        def chain(engine, instruction):
            instruction.then_inc(s_w, 1)
            step[0] += 1

        def after_chain(engine):
            engine.wait_ge(s_w, step[0])

        dve.wait_ge(s_ld, n_ld)
        dve.memset(v_one[:, :, :, :], 1.0)
        dve.memset(ps_o[:, :, :], 0.0)
        dve.memset(minus_half[:, :], -0.5)
        dve.memset(eps[:, :], EPS)
        dve.memset(ones[:, :], 1.0)
        dve.tensor_copy(ident_b[:, :], ident[:, :])
        dve.tensor_scalar(wq_nat[:, 0:2, :], wq_nat[:, 0:2, :], SCALE, None, ALU.mult)
        chain(dve, dve.tensor_scalar(slope8[:, :], slope8[:, :], MAX_BIAS, None, ALU.mult))
        after_chain(dve)
        for h in range(H):
            ins = dve.tensor_scalar(alibi[:, h, :], toep[:, 0:U_W], slope8[:, h:h + 1], None, ALU.mult)
        chain(dve, ins)
        s8 = slope8[M_ROW:P, :]
        chain(dve, dve.tensor_copy(partb[:, 0, :], s8)); after_chain(dve)
        chain(dve, dve.tensor_tensor(part[:, 3, :], s8, partb[:, 0, :], ALU.subtract)); after_chain(dve)
        chain(dve, dve.tensor_copy(partb[:, 1, :], part[:, 3, :])); after_chain(dve)
        chain(dve, dve.tensor_tensor(part[:, 4, :], part[:, 3, :], partb[:, 1, :], ALU.subtract)); after_chain(dve)
        chain(dve, dve.tensor_copy(partb[:, 2, :], part[:, 4, :])); after_chain(dve)
        for s in range(2):
            chain(dve, dve.tensor_scalar(side[:, s, :], partb[:, 0, :], pick[:, 4 * s:4 * s + 1],
                                         pick[:, 4 * s + 3:4 * s + 4], ALU.mult, ALU.add)); after_chain(dve)
            for i in (1, 2):
                chain(dve, dve.scalar_tensor_tensor(out=side[:, s, :], in0=partb[:, i, :],
                                                    scalar=pick[:, 4 * s + i:4 * s + i + 1], in1=side[:, s, :],
                                                    op0=ALU.mult, op1=ALU.add)); after_chain(dve)
        chain(dve, dve.tensor_tensor(side[:, 1, :], side[:, 1, :], pick[:, 8:8 + H], ALU.add)); after_chain(dve)
        for h in range(H):
            for s in range(2):
                ins = dve.tensor_scalar(at[M_ROW:P, h, s, :], pat[:, s, :], side[:, s, h:h + 1], None, ALU.mult)
        chain(dve, ins)

        ps_m0 = ps_misc[:, 0, :]
        after_chain(pe)
        pe.wait_ge(s_ld, n_ld)
        flat_t = ps_t[:, :, :].rearrange("p a n -> p (a n)")
        for kc in range(KC):
            for a in range(6):
                pe.transpose(flat_t[:, (kc * 6 + a) * P:(kc * 6 + a + 1) * P],
                             wq_nat[:, a, kc * P:(kc + 1) * P], ident[:, :])
        for kc in range(KC):
            for a in range(2):
                pe.transpose(ps_s[:, kc, a * P:(a + 1) * P], proj_nat[:, a, kc * P:(kc + 1) * P], ident[:, :])
        for a in range(2):
            pe.transpose(ps_m0[0:R_LORA, a * P:(a + 1) * P], vr_nat[:, a, :], ident[:, :])
        for a in range(2):
            ins = pe.transpose(ps_m0[0:R_LORA, C + a * P:C + (a + 1) * P], cr_nat[:, a, :], ident[:, :])
        chain(pe, ins)
        after_chain(dve)
        for kc in range(KC):
            dve.tensor_copy(wqkv_t[:, kc, :], flat_t[:, kc * 3 * C:(kc + 1) * 3 * C])
            dve.tensor_copy(proj_t[:, kc, :], ps_s[:, kc, 0:C])
        chain(dve, dve.tensor_copy(vc_t, ps_m0[0:R_LORA, :]))
        after_chain(pe)
        for kc in range(KC):
            for a in range(2):
                dst = ps_m0[:, kc * C + a * P:kc * C + (a + 1) * P]
                pe.matmul(dst, vc_t[:, kc * P:(kc + 1) * P], vc_t[:, C + a * P:C + (a + 1) * P],
                          start=True, stop=False)
                ins = pe.matmul(dst, w_nat[:, a, kc * P:(kc + 1) * P], ident[:, :], start=False, stop=True)
        chain(pe, ins)
        after_chain(dve)
        chain(dve, dve.tensor_copy(ffn_t[:, :, :].rearrange("p a b -> p (a b)"), ps_m0[:, :]))
        for engine in (pe, act, pool, sp, dve):
            after_chain(engine)

        e_load = event("e_load", 1, 16)
        e_aggr = event("e_aggr", 1)
        e_bn = event("e_bn", 1)
        e_veps = event("e_veps", 1)
        e_rstd = event("e_rstd", 1)
        e_xhat = event("e_xhat", 1)
        e_xt = event("e_xt", KC)
        e_rope = event("e_rope", G)
        e_qk = event("e_qk", G)
        e_hi = event("e_hi", G)
        e_r1 = event("e_r1", G)
        e_mid = event("e_mid", G)
        e_lo = event("e_lo", G)
        e_rep = event("e_rep", G)
        e_at = event("e_at", H)
        e_vs = event("e_vs", 2)
        e_v1 = event("e_v1", G)
        e_s = event("e_s", H * T)
        e_mx = event("e_mx", H * T)
        e_mhi = event("e_mhi", G)
        e_m2 = event("e_m2", G)
        e_mt = event("e_mt", G)
        e_mrow = event("e_mrow", G, 16)
        e_st = event("e_st", H * T)
        e_dg = event("e_dg", H * T)
        e_ex = event("e_ex", H * T)
        e_pv = event("e_pv", H)
        e_o = event("e_o", G)
        e_rden = event("e_rden", G)
        e_att = event("e_att", G)
        e_res = event("e_res", 1, 16)
        e_resb = event("e_resb", 1)
        e_aT = event("e_aT", KC)
        e_x1 = event("e_x1", 2)
        e_bn2 = event("e_bn2", 1)
        e_aggr2 = event("e_aggr2", 1)
        e_veps2 = event("e_veps2", 1)
        e_rstd2 = event("e_rstd2", 1)
        e_xhat2 = event("e_xhat2", 1)
        e_x1b = event("e_x1b", 1)
        e_x2t = event("e_x2t", KC)
        e_y = event("e_y", 2)
        e_out = event("e_out", 1, 16)
        misc = MiscBanks(sem("misc_full"))

        def load_x(b):
            e_xhat.wait(sp, b.before(), 1)
            sp.dma_start(x_in[:, :, :], x[b.index()].rearrange("(t p) c -> p t c", p=P)) \
              .then_inc(e_load.sem, 16)

        def ln_stats(b, src, ln, bn, aggr, veps, rs):
            for t in range(T):
                ins = dve.bn_stats(stats[:, ln, t, :], src[:, t, :])
            bn.mark(ins)
            bn.wait(dve, b, 1)
            dve.nop(nofuse=True)
            for t in range(T):
                ins = dve.bn_aggr(mean_var[:, ln, t, :], stats[:, ln, t, :])
            aggr.mark(ins)
            aggr.wait(pool, b, 1)
            veps.mark(pool.tensor_tensor(var_eps[:, ln, :], mean_var[:, ln, :, 1], eps[:, :], ALU.add))
            veps.wait(pool, b, 1)
            rs.mark(pool.tensor_tensor(rstd[:, ln, :], var_eps[:, ln, :], minus_half[:, :], ALU.pow))

        def stats1(b):
            e_load.wait(dve, b, 1)
            ln_stats(b, x_in, 0, e_bn, e_aggr, e_veps, e_rstd)

        def normalise(b, src, dst, ln, rs, done):
            rs.wait(dve, b, 1)
            for t in range(T):
                ins = dve.tensor_scalar(dst[:, t, :], src[:, t, :], mean_var[:, ln, t, 0:1], rstd[:, ln, t:t + 1],
                                        ALU.subtract, ALU.mult)
            done.mark(ins)

        def transpose_tokens(b, kc, src, dst, ready, ready_n, done):
            bank = ps_misc[:, misc.fill(pe), :]
            ready.wait(pe, b, ready_n)
            for t in range(T):
                ins = pe.transpose(bank[:, t * P:(t + 1) * P], src[:, t, kc * P:(kc + 1) * P], ident[:, :])
            unit = misc.filled(ins, done, b, kc + 1)
            yield
            misc.wait_full(act, b, unit)
            done.mark(act.copy(dst[:, kc, :], bank))

        def project_qk(b, g):
            w0 = HG * D
            bank = ps_misc[:, misc.fill(pe), :]
            if g == 0:
                e_xt.wait(pe, b, KC)
            for t in range(T):
                if t:
                    yield
                for kc in range(KC):
                    wt = wqkv_t[:, kc, 0:2 * C].rearrange("p (s o) -> p s o", s=2)[:, :, g * w0:(g + 1) * w0]
                    dst = bank.rearrange("p (s t o) -> p s t o", s=2, t=T)[:, :, t, :]
                    ins = pe.matmul(dst, xt[:, kc, t * P:(t + 1) * P], wt, start=(kc == 0), stop=(kc == KC - 1))
            unit = misc.filled(ins, e_rope, b, g + 1)
            yield
            misc.wait_full(dve, b, unit)
            prev = (b, g) if g else (b.before(), G)
            e_qk.wait(dve, *prev)
            m2 = bank.rearrange("p (s n) -> p s n", s=2)
            m4 = bank.rearrange("p (s n d) -> p s n d", s=2, d=D)
            b4 = rope_b[:, :, :].rearrange("p s (n d) -> p s n d", d=D)
            s4 = rope_sin[:, :].rearrange("p (o n d) -> p o n d", o=1, d=D)
            cos2 = rope_cos[:, :].rearrange("p (o n) -> p o n", o=1).broadcast_to([P, 2, T * HG * D])
            hd = D // 2
            dve.tensor_tensor(rope_a[:, :, :], m2, cos2, ALU.mult)
            for lo, hi in ((0, hd), (hd, 0)):
                ins = dve.tensor_tensor(b4[:, :, :, lo:lo + hd], m4[:, :, :, hi:hi + hd],
                                        s4[:, :, :, lo:lo + hd].broadcast_to([P, 2, T * HG, hd]), ALU.mult)
            e_rope.mark(ins)
            e_rope.wait(pool, b, g + 1)
            e_qk.mark(pool.tensor_tensor(rope_a[:, :, :], rope_a[:, :, :], rope_b[:, :, :], ALU.add))

        def parts(g):
            return qka[:, g % 2, :, :, :, :, :].rearrange("p s t h e d -> p (s t h) e d")

        a3 = rope_a[:, :, :].rearrange("p s (n d) -> p (s n) d", d=D)
        r3 = rest1[:, :, :].rearrange("p s (n d) -> p (s n) d", d=D)

        def high_parts(b, g):
            q5 = parts(g)
            e_qk.wait(act, b, g + 1)
            e_hi.mark(act.copy(q5[:, :, 0, :], a3))
            e_hi.wait(pool, b, g + 1)
            e_r1.mark(pool.tensor_tensor(r3, a3, q5[:, :, 0, :], ALU.subtract))

        def middle_parts(b, g):
            q5 = parts(g)
            e_r1.wait(act, b, g + 1)
            e_mid.mark(act.copy(q5[:, :, 1, :], r3))
            e_mid.wait(pool, b, g + 1)
            n = T * HG
            pool.tensor_tensor(q5[:, 0:n, 5, :], r3[:, 0:n, :], q5[:, 0:n, 1, :], ALU.subtract)
            e_lo.mark(pool.tensor_tensor(q5[:, n:2 * n, 4, :], r3[:, n:2 * n, :], q5[:, n:2 * n, 1, :],
                                         ALU.subtract))

        def repeat_parts(b, g):
            par, n = g % 2, T * HG
            q5 = qka[:, par, :, :, :, :, :].rearrange("p s t h e d -> p (s t h) e d")
            e_mid.wait(dve, b, g + 1)
            dve.tensor_copy(q5[:, 0:n, 2:5:2, :], q5[:, 0:n, 0:1, :].broadcast_to([P, n, 2, D]))
            dve.tensor_copy(q5[:, n:2 * n, 3:6:2, :], q5[:, n:2 * n, 0:1, :].broadcast_to([P, n, 2, D]))
            dve.tensor_copy(q5[:, 0:n, 3, :], q5[:, 0:n, 1, :])
            e_rep.mark(dve.tensor_copy(q5[:, n:2 * n, 2, :], q5[:, n:2 * n, 1, :]))

        def operands(b, h):
            g, hh = divmod(h, HG)
            bank = ps_misc[:, misc.fill(pe), :]
            if hh == 0:
                e_lo.wait(pe, b, g + 1)
                e_rep.wait(pe, b, g + 1)
            for s in range(2):
                if s:
                    yield
                for t in range(T):
                    ins = pe.transpose(bank.bitcast(BF16)[0:QK_ROWS, s * N + t * P:s * N + (t + 1) * P],
                                       qka[:, g % 2, s, t, hh, :, :].rearrange("p e d -> p (e d)"), ident_b[:, :])
            unit = misc.filled(ins, e_at, b, h + 1)
            yield
            misc.wait_full(act, b, unit)
            for s in range(2):
                if s:
                    yield
                ins = act.copy(at[0:QK_ROWS, h, s, :], bank.bitcast(BF16)[0:QK_ROWS, s * N:(s + 1) * N])
            e_at.mark(ins)

        def project_v(b, u):
            bank = ps_misc[:, misc.fill(pe), :]
            if u == 0:
                e_xt.wait(pe, b, KC)
            for t in (2 * u, 2 * u + 1):
                for kc in range(KC):
                    if t % 2 or kc:
                        yield
                    ins = pe.matmul(bank[:, (t % 2) * C:(t % 2 + 1) * C], xt[:, kc, t * P:(t + 1) * P],
                                    wqkv_t[:, kc, 2 * C:3 * C], start=(kc == 0), stop=(kc == KC - 1))
            unit = misc.filled(ins, e_vs, b, u + 1)
            yield
            misc.wait_full(act, b, unit)
            e_v1.wait(act, b.before(), G)
            e_vs.mark(act.copy(v_stage[:, 2 * u:2 * u + 2, :].rearrange("p t c -> p (t c)"), bank))

        def place_v(b, g):
            e_vs.wait(pool, b, 2)
            e_pv.wait(pool, b.before(), HG * (g + 1))
            one = ones[:, :].rearrange("p (a b c) -> p a b c", a=1, b=1).broadcast_to([P, T, HG, D])
            e_v1.mark(pool.tensor_tensor(
                v_one[:, :, g * HG:(g + 1) * HG, 0:D],
                v_stage[:, :, g * HG * D:(g + 1) * HG * D].rearrange("p t (h d) -> p t h d", d=D), one, ALU.mult))

        def max_scores(b, h, t):
            if t == 0:
                e_at.wait(pe, b, h + 1)
            k = h * T + t
            e_mx.wait(pe, b, k - 1)
            e_s.mark(pe.matmul(ps_s[:, t % 2, :], at[0:QK_ROWS, h, 0, t * P:(t + 1) * P],
                               at[0:QK_ROWS, h, 1, :], start=True, stop=True))

        def row_maximum(b, h, t):
            k = h * T + t
            g, hh = divmod(h, HG)
            if h % HG == 0 and t == 0:
                e_m2.wait(dve, *((b, g - 1) if g >= 2 else (b.before(), G + g - 1)))
            e_s.wait(dve, b, k + 1)
            dve.nop(nofuse=True)
            off = (T - 1 - t) * P
            e_mx.mark(dve.tensor_tensor_reduce(junk[:, t, :], ps_s[:, t % 2, :], alibi[:, h, off:off + N], 1.0, LOWEST,
                                               ALU.add, ALU.max, row_max[:, g % 2, t, hh:hh + 1]))

        def split_max(b, g):
            e_mx.wait(pool, b, (g + 1) * HG * T)
            e_mrow.wait(pool, *((b, g) if g else (b.before(), G)))
            one = ones[:, :].rearrange("p (a b) -> p a b", a=1).broadcast_to([P, T, HG])
            e_mhi.mark(pool.tensor_tensor(max2[:, :, :, 0], row_max[:, g % 2, :, :], one, ALU.mult))
            e_mhi.wait(pool, b, g + 1)
            e_m2.mark(pool.tensor_tensor(max2[:, :, :, 1], row_max[:, g % 2, :, :], max2[:, :, :, 0],
                                         ALU.subtract))

        def max_rows(b, g):
            bank = ps_misc[:, misc.fill(pe), :]
            e_m2.wait(pe, b, g + 1)
            for t in range(T):
                ins = pe.transpose(bank.bitcast(BF16)[M_ROW:BIAS_ROW, t * P:(t + 1) * P],
                                   max2[:, t, :, :].rearrange("p h e -> p (h e)"), ident_b[:, :])
            unit = misc.filled(ins, e_mt, b, g + 1)
            yield
            misc.wait_full(act, b, unit)
            if g == 0:
                e_mrow.wait(act, b.before(), G)
            else:
                e_mrow.wait(act, b, g)
            e_mt.mark(act.copy(max_t[M_ROW:BIAS_ROW, :], bank.bitcast(BF16)[M_ROW:BIAS_ROW, 0:N]))
            e_mt.wait(sp, b, g + 1)
            src = max_t[M_ROW:BIAS_ROW, :].rearrange("p (o n) -> p o n", o=1).broadcast_to([2 * HG, HG, N])
            sp.dma_start(at[M_ROW:BIAS_ROW, g * HG:(g + 1) * HG, 0, :], src).then_inc(e_mrow.sem, 16)

        def exp_scores(b, h, j):
            k = T * h + j
            if h % HG == 0 and j == 0:
                e_mrow.wait(pe, b, h // HG + 1)
            last = k - T_BANKS if k >= T_BANKS else max(n for n in range(H * T) if n % T_BANKS == k)
            e_ex.wait(pe, b if k >= T_BANKS else b.before(), last + 1)
            e_st.mark(pe.matmul(ps_t[:, k % T_BANKS, :], at[:, h, 1, j * P:(j + 1) * P], at[:, h, 0, :],
                                start=True, stop=True))

        def diagonal_bias(b, h, j):
            k = T * h + j
            e_st.wait(dve, b, k + 1)
            block = ps_t[:, k % T_BANKS, j * P:(j + 1) * P]
            e_dg.mark(dve.scalar_tensor_tensor(out=block, in0=diag[:, :], scalar=slope8[:, h:h + 1], in1=block,
                                               op0=ALU.mult, op1=ALU.add))

        def exponentials(b, h, j):
            k = T * h + j
            e_dg.wait(act, b, k + 1)
            if j == 0:
                e_pv.wait(act, b, h - 1)
            e_ex.mark(act.activation(pt[:, h % 2, j, :], ps_t[:, k % T_BANKS, :], ACT.Exp))

        def weighted_values(b, h):
            g, hh = divmod(h, HG)
            if hh == 0:
                e_v1.wait(pe, b, g + 1)
                e_o.wait(pe, *((b, g) if g else (b.before(), G)))
            for j in range(T):
                if j:
                    yield
                e_ex.wait(pe, b, T * h + j + 1)
                for t in range(T):
                    ins = pe.matmul(ps_o[32 * t:32 * t + D + 1, hh, :], v_one[:, j, h, 0:D + 1],
                                    pt[:, h % 2, j, t * P:(t + 1) * P], start=(j == 0), stop=(j == T - 1),
                                    skip_group_check=True)
            e_pv.mark(ins)

        def o_out(b, g):
            e_pv.wait(act, b, HG * (g + 1))
            e_att.wait(act, *((b, g) if g else (b.before(), G)))
            e_o.mark(act.copy(o_sb[:, :, :], ps_o[:, :, :]))

        def attention_out(b, g):
            bank = ps_misc[:, misc.fill(pe), :]
            e_o.wait(pe, b, g + 1)
            for hh in range(HG):
                ins = pe.transpose(bank[:, hh * P:(hh + 1) * P], o_sb[:, hh, :], ident[:, :])
            unit = misc.filled(ins, e_att, b, g + 1)
            yield
            misc.wait_full(dve, b, unit)
            o4 = bank.rearrange("p (h t d) -> p h t d", h=HG, t=T)
            e_rden.mark(dve.reciprocal(r_den[:, :, :], o4[:, :, :, D]))
            e_rden.wait(dve, b, g + 1)
            if g == 0:
                e_aT.wait(dve, b.before(), KC)
            dst = attn[:, :, g * HG * D:(g + 1) * HG * D].rearrange("p t (h d) -> p h t d", d=D)
            den = r_den[:, :, :].rearrange("p h (t o) -> p h t o", o=1).broadcast_to([P, HG, T, D])
            e_att.mark(dve.tensor_tensor(dst, o4[:, :, :, 0:D], den, ALU.mult))

        def load_residual(b):
            e_x1.wait(sp, b.before(), 2)
            sp.dma_start(x_res[:, :, :], x[b.index()].rearrange("(t p) c -> p t c", p=P)) \
              .then_inc(e_res.sem, 16)

        def residual_bias(b):
            e_res.wait(pool, b, 1)
            bias = proj_bias[:, :].rearrange("p (o c) -> p o c", o=1).broadcast_to([P, T, C])
            e_resb.mark(pool.tensor_tensor(x_res[:, :, :], x_res[:, :, :], bias, ALU.add))

        def out_projection(b, u):
            bank = ps_misc[:, misc.fill(pe), :]
            if u == 0:
                e_aT.wait(pe, b, KC)
            for t in (2 * u, 2 * u + 1):
                for kc in range(KC):
                    if t % 2 or kc:
                        yield
                    ins = pe.matmul(bank[:, (t % 2) * C:(t % 2 + 1) * C], attn_t[:, kc, t * P:(t + 1) * P],
                                    proj_t[:, kc, :], start=(kc == 0), stop=(kc == KC - 1))
            unit = misc.filled(ins, e_x1, b, u + 1)
            yield
            misc.wait_full(dve, b, unit)
            if u == 0:
                e_resb.wait(dve, b, 1)
            two = slice(2 * u, 2 * u + 2)
            e_x1.mark(dve.tensor_tensor(x1[:, two, :], bank.rearrange("p (t c) -> p t c", t=2),
                                        x_res[:, two, :], ALU.add))

        def stats2(b):
            e_x1.wait(dve, b, 2)
            ln_stats(b, x1, 1, e_bn2, e_aggr2, e_veps2, e_rstd2)
            e_out.wait(pool, b.before(), 1)
            bias = ffn_bias[:, :].rearrange("p (o c) -> p o c", o=1).broadcast_to([P, T, C])
            e_x1b.mark(pool.tensor_tensor(y[:, :, :], x1[:, :, :], bias, ALU.add))

        def second_linear(b, u):
            bank = ps_misc[:, misc.fill(pe), :]
            if u == 0:
                e_x2t.wait(pe, b, KC)
            for t in (2 * u, 2 * u + 1):
                for kc in range(KC):
                    if t % 2 or kc:
                        yield
                    ins = pe.matmul(bank[:, (t % 2) * C:(t % 2 + 1) * C], x2t[:, kc, t * P:(t + 1) * P],
                                    ffn_t[:, kc, :], start=(kc == 0), stop=(kc == KC - 1))
            unit = misc.filled(ins, e_y, b, u + 1)
            yield
            misc.wait_full(dve, b, unit)
            if u == 0:
                e_x1b.wait(dve, b, 1)
            two = slice(2 * u, 2 * u + 2)
            e_y.mark(dve.tensor_tensor(y[:, two, :], bank.rearrange("p (t c) -> p t c", t=2),
                                       y[:, two, :], ALU.add))

        def store(b):
            e_y.wait(sp, b, 2)
            sp.dma_start(out[b.index()].rearrange("(t p) c -> p t c", p=P), y[:, :, :]).then_inc(e_out.sem, 16)

        pieces = []

        def put(slot, places, piece, *args):
            pieces.append((slot + SHIFT, places, piece, args))

        heavy2, heavy4 = (8, 16, 33, 38, 46), (8, 16, 33, 38, 46)
        put(S_LOAD, (0,), load_x)
        put(S_STAT, (48,), stats1)
        put(S_NORM, (80,), lambda b: normalise(b, x_in, x_hat, 0, e_rstd, e_xhat))
        for kc in range(KC):
            put(S_XT, (6 + 25 * kc, 22 + 25 * kc), lambda b, kc=kc: transpose_tokens(b, kc, x_hat, xt, e_xhat, 1, e_xt))
        for g in range(G):
            put(S_G0 + HG * g, heavy4, project_qk, g)
            put(S_G0 + HG * g + 1, (24,), high_parts, g)
            put(S_G0 + HG * g + 1, (74,), middle_parts, g)
            put(S_G0 + HG * g + 2, (12,), repeat_parts, g)
            put(S_VCOPY0 + HG * g, (50,), place_v, g)
            put(S_MS0 + HG * g - 1, (98,), split_max, g)
            put(S_MS0 + HG * g, (90, 94), max_rows, g)
            put(S_O0 + HG * g - 2, (98,), o_out, g)
            put(S_O0 + HG * g, (80, 88), attention_out, g)
        for u in range(2):
            put(S_V + 2 * u, heavy2, project_v, u)
            put(S_F2 + u, heavy2, out_projection, u)
            put(S_F4 + u, heavy2, second_linear, u)
        for h in range(H):
            put(S_U0 + h, (57, 59, 62, 69), operands, h)
            put(S_PV0 + h, (30, 48, 64, 82), weighted_values, h)
            for t in range(T):
                put(h, (25 * t,), max_scores, h, t)
                put(h, (25 * t + 1,), row_maximum, h, t)
            for j in range(T):
                put(S_E0 + h, (25 * j + 5,), exp_scores, h, j)
                put(S_E0 + h, (25 * j + 20,), diagonal_bias, h, j)
                put(S_E0 + h, (25 * j + 21,), exponentials, h, j)
        for kc in range(KC):
            put(S_F1 + kc, (82, 92), lambda b, kc=kc: transpose_tokens(b, kc, attn, attn_t, e_att, G, e_aT))
            put(S_F3, (6 + 25 * kc, 22 + 25 * kc),
                lambda b, kc=kc: transpose_tokens(b, kc, x_hat2, x2t, e_xhat2, 1, e_x2t))
        put(S_RES, (0,), load_residual)
        put(S_RESB, (50,), residual_bias)
        put(S_LN2, (2,), stats2)
        put(S_LN2, (60,), lambda b: normalise(b, x1, x_hat2, 1, e_rstd2, e_xhat2))
        put(S_F4 + 1, (52,), store)
        assert max(p[0] for p in pieces) < DEPTH * SLOTS and min(p[0] for p in pieces) >= 0

        def body(i, alive):
            for slot in range(SLOTS):
                now = [p for p in pieces if p[0] % SLOTS == slot and p[0] // SLOTS in alive]
                parts_of = sorted((place, n, k) for n, p in enumerate(now) for k, place in enumerate(p[1]))
                runs = {}
                for _, n, k in parts_of:
                    at_slot, places, piece, args = now[n]
                    if k == 0:
                        runs[n] = piece(Batch(i, at_slot // SLOTS), *args)
                    if runs[n] is not None:
                        done = next(runs[n], "end") == "end"
                        assert done == (k == len(places) - 1), piece

        for i in range(DEPTH):
            body(i, [d for d in range(DEPTH) if 0 <= i - d < NB])

        units = sum(len(p[1]) > 1 for p in pieces if p[2] is not weighted_values)
        before, last = misc.n, misc.emptied
        with nc.Fori(DEPTH, NB) as i:
            misc.slope, misc.base, misc.n = units, before - units * DEPTH, 0
            misc.first = before % MiscBanks.BANKS
            misc.emptied = [(ev, Batch(i, b.d + 1), k) for ev, b, k in last]
            body(i, range(DEPTH))
            assert misc.n == units and units % MiscBanks.BANKS == 0
            assert [(ev, b.d, k) for ev, b, k in misc.emptied] == [(ev, b.d, k) for ev, b, k in last]
        misc.first, misc.slope, misc.base, misc.n = 0, 0, 0, before + units * (NB - DEPTH)
        misc.emptied = [(ev, Batch(NB - 1, b.d), k) for ev, b, k in last]
        for i in range(NB, NB + DEPTH - 1):
            body(i, [d for d in range(DEPTH) if 0 <= i - d < NB])
        e_out.wait(sp, Batch(NB - 1, 0), 1)


_INS = ["L0_attn_x", "L0_attn_qkv_w", "L0_attn_proj_w", "L0_attn_proj_b", "L0_attn_slopes",
        "L0_ffn_W", "L0_ffn_b", "L0_ffn_V_r", "L0_ffn_C"]


def kernel(**inputs):
    import numpy as _np
    import concourse.bacc as _bacc
    from concourse import mybir as _mybir
    from concourse.bass_utils import run_bass_kernel_spmd as _run

    nc = _bacc.Bacc("TRN2", target_bir_lowering=False, num_devices=1)
    arrays, args, consts = {}, [], {}
    for name in _INS:
        a = _np.ascontiguousarray(inputs[name])
        arrays[f"in_{name}_dram"] = a
        args.append(nc.dram_tensor(f"in_{name}_dram", a.shape, _mybir.dt.from_np(a.dtype),
                                   kind="ExternalInput").ap())
    for name, a in shape_constants().items():
        a = _np.ascontiguousarray(a)
        arrays[f"const_{name}_dram"] = a
        consts[name] = nc.dram_tensor(f"const_{name}_dram", a.shape, _mybir.dt.from_np(a.dtype),
                                      kind="ExternalInput").ap()
    out = nc.dram_tensor("out_dram", (NB, N, C), _mybir.dt.float32, kind="ExternalOutput").ap()
    layer(nc, *args, consts, out)
    r = _run(nc, [arrays], core_ids=[0])
    return r.results[0]["out_dram"]
```

```python
from contextlib import ExitStack

import numpy as np
import concourse.bass as bass
from concourse import mybir

F32 = mybir.dt.float32
BF16 = mybir.dt.bfloat16
ALU = mybir.AluOpType
ACT = mybir.ActivationFunctionType

P = 128
NB, N, C = 32, 512, 256
H, D = 16, 16
T = N // P
KC = C // P
HG = 4
G = H // HG
R_LORA = 32
MAX_BIAS = 8.0
SCALE = float(D) ** -0.5
EPS = 1e-5
LOWEST = -3.0e38

QK_ROWS = 6 * D
M_ROW = QK_ROWS
BIAS_ROW = M_ROW + 2 * HG
U_W = N + (T - 1) * P

WHEN = {
    "load_x": (-12, (0,)), "stats1": (-11, (67.6,)), "norm1": (-10, (80,)), "xt0": (-8, (6, 22)),
    "xt1": (-8, (27.7, 43.7)),
    "project_qk": (-5, (24.4, 32.4, 49.4, 54.4, 62.4)), "high": (-4, (26,)), "middle": (-4, (63.6,)),
    "repeat": (-3, (12, 34)),
    "v0": (-6, (8, 16, 33, 38, 46)), "v1": (-4, (13.5, 21.5, 38.5, 43.5, 51.5)), "place_v": (-2, (53.6,)),
    "operands": (-2, (57, 59, 62, 69)),
    "s": (0, (0, 11.5, 36.5, 61.5)), "r": (0, (0, 22, 47, 71)),
    "split_max": (4, (81.3,)), "max_rows": (5, (90, 94)),
    "t": (7, (5, 30, 55, 80)), "d": (7, (20, 26.5, 70, 95)), "e": (7, (21, 46, 71, 96)),
    "pv": (8, (46.1, 64.1, 80.1, 98.1)), "o_out": (11, (93,)), "attention_out": (13, (80, 88)),
    "load_residual": (20, (0,)), "residual_bias": (22, (50,)), "f1a": (26, (82, 92)), "f1b": (27, (87.1, 97.1)),
    "f2a": (29, (12.2, 20.2, 37.2, 42.2, 50.2)), "f2b": (30, (15.4, 23.4, 40.4, 45.4, 53.4)),
    "stats2": (30, (65,)), "norm2": (31, (20,)), "f3a": (32, (6, 22)), "f3b": (32, (11.5, 27.5)),
    "f4a": (33, (16, 16.6, 33, 38, 46)), "f4b": (34, (8, 16, 33, 38, 46)), "store": (34, (52,)),
    "load_tables": (-12, (10.4,)), "slope_parts": (-9, (0,)), "alibi_table": (-8, (90,)),
    "constant_rows": (-1, (99,)),
}
SLOTS = H
T_BANKS = 3
DEPTH = 3


def shape_constants():
    f = np.float32
    inv_freq = (f(1.0) / np.power(f(10000.0), np.arange(0, D, 2, dtype=f) / f(D))).astype(f)
    freqs = (np.arange(N, dtype=f)[:, None] * inv_freq[None, :]).astype(f)
    sin, cos = np.sin(freqs.astype(np.float64)).astype(f), np.cos(freqs.astype(np.float64)).astype(f)

    def tile(a):
        return np.repeat(a.reshape(T, P, 1, -1), HG, axis=2).transpose(1, 0, 2, 3)

    rope_cos = tile(np.concatenate([cos, cos], 1)).reshape(P, -1)
    rope_sin = tile(np.concatenate([-sin, sin], 1)).reshape(P, -1)
    q = np.arange(P, dtype=f)[:, None]
    toep = np.minimum(np.arange(U_W, dtype=f)[None, :] - (U_W - N) - q, 0).astype(f)
    diag = np.minimum(q - np.arange(P, dtype=f)[None, :], 0).astype(f)
    rows = P - M_ROW
    kpat, qpat = np.zeros((rows, N), f), np.zeros((rows, N), f)
    kpick, qpick = np.zeros((rows, 4), f), np.zeros((rows, 4), f)
    tile_of, within = np.arange(N) // P, np.arange(N) % P
    kpat[0:2 * HG] = 1.0
    r = BIAS_ROW - M_ROW
    for j in range(T - 1):
        later, mine = (tile_of > j).astype(f), (tile_of == j).astype(f)
        for part in range(3):
            kpat[r], qpat[r] = mine, -later * (within + 1)
            kpick[r, part], qpick[r, 3] = 1, 1
            r += 1
        for part in range(3):
            kpat[r], qpat[r] = mine * (P - 1 - within), -later
            kpick[r, 3], qpick[r, part] = 1, 1
            r += 1
        if j < T - 2:
            for part in range(3):
                kpat[r], qpat[r] = mine, -later * P * (tile_of - j - 1)
                kpick[r, part], qpick[r, 3] = 1, 1
                r += 1
    assert r == rows
    mrow = np.zeros((rows, H), f)
    for h in range(H):
        mrow[2 * (h % HG):2 * (h % HG) + 2, h] = -1.0
    return {"rope_cos": rope_cos, "rope_sin": rope_sin, "toep": toep, "diag": diag,
            "pat": np.stack([qpat, kpat], 1).reshape(rows, -1), "pick": np.concatenate([qpick, kpick, mrow], 1),
            "ident": np.eye(P, dtype=f)}


class Batch:

    def __init__(self, i, d):
        self.i, self.d = i, d

    def before(self):
        return Batch(self.i, self.d + 1)

    def index(self):
        return self.i - self.d

    def is_first(self):
        return isinstance(self.i, int) and self.index() == 0


class Event:

    def __init__(self, sem, per, step=1):
        self.sem, self.per, self.step = sem, per, step

    def mark(self, instruction):
        instruction.then_inc(self.sem, self.step)

    def wait(self, engine, b, k):
        rest = (k - b.d * self.per) * self.step
        if isinstance(b.i, int):
            value = b.i * self.per * self.step + rest
            if value > 0:
                engine.wait_ge(self.sem, value)
        else:
            engine.wait_ge(self.sem, b.i * (self.per * self.step) + rest)


class MiscBanks:

    BANKS = 2

    def __init__(self, full):
        self.full = full
        self.base, self.slope, self.n = 0, 0, 0
        self.first = 0
        self.emptied = []

    def fill(self, pe):
        if len(self.emptied) == self.BANKS:
            ev, b, k = self.emptied[0]
            ev.wait(pe, b, k)
        return (self.first + self.n) % self.BANKS

    def filled(self, matmul, ev, b, k):
        matmul.then_inc(self.full, 1)
        self.n += 1
        self.emptied = self.emptied[-(self.BANKS - 1):] + [(ev, b, k)]
        return self.n

    def wait_full(self, engine, b, unit):
        engine.wait_ge(self.full, b.i * self.slope + (self.base + unit) if self.slope else self.base + unit)


def layer(nc, x, qkv_w, proj_w, proj_b, slopes, w, wb, v_r, c_r, consts, out):
    pe, dve, act, pool, sp = nc.tensor, nc.vector, nc.scalar, nc.gpsimd, nc.sync
    ctx = ExitStack()
    with ctx:
        def sb(name, shape, dt=F32):
            return ctx.enter_context(nc.sbuf_tensor(name, shape, dt))

        def ps(name, shape, dt=F32):
            return ctx.enter_context(nc.psum_tensor(name, shape, dt))

        def sem(name):
            return ctx.enter_context(nc.semaphore(name))

        def event(name, per, step=1):
            return Event(sem(name), per, step)

        ident = sb("ident", [P, P])
        ident_b = sb("ident_b", [P, P], BF16)
        rope_cos = sb("rope_cos", [P, T * HG * D])
        rope_sin = sb("rope_sin", [P, T * HG * D])
        diag = sb("diag", [P, P])
        alibi = sb("alibi", [P, H, U_W])
        slope8 = sb("slope8", [P, H])
        wqkv_t = sb("wqkv_t", [P, KC, 3 * C])
        proj_t = sb("proj_t", [P, KC, C])
        ffn_t = sb("ffn_t", [P, KC, C])
        proj_bias = sb("proj_bias", [P, C])
        ffn_bias = sb("ffn_bias", [P, C])
        minus_half = sb("minus_half", [P, T])
        eps = sb("eps", [P, T])
        ones = sb("ones", [P, 1])
        bias_rows = sb("bias_rows", [P, 2 + 2, H])
        slope_bf = sb("slope_bf", [P, 3, H], BF16)
        row_pick = sb("row_pick", [P, 8 + H])
        side, rest = bias_rows[M_ROW:P, 0:2, :], bias_rows[M_ROW:P, 2:4, :]
        partb, pick = slope_bf[M_ROW:P, :, :], row_pick[M_ROW:P, :]

        x_in = sb("x_in", [P, T, C])
        stats = sb("stats", [P, 2, T, 6])
        mean_var = sb("mean_var", [P, 2, T, 2])
        var_eps = sb("var_eps", [P, 2, T])
        rstd = sb("rstd", [P, 2, T])
        x_hat = sb("x_hat", [P, T, C])
        xt = sb("xt", [P, KC, N])
        rope_a = sb("rope_a", [P, 2, T * HG * D])
        rope_b = sb("rope_b", [P, 2, T * HG * D])
        rest1 = sb("rest1", [P, 2, T * HG * D])
        qka = sb("qka", [P, 2, 2, T, HG, 6, D], BF16)
        at = sb("at", [P, H, 2, N], BF16)
        v_stage = sb("v_stage", [P, T, C])
        v_one = sb("v_one", [P, T, H, 32])
        row_max = sb("row_max", [P, 2, T, HG])
        max2 = sb("max2", [P, T, HG, 2], BF16)
        max_t = sb("max_t", [P, N], BF16)
        junk = sb("junk", [P, T, N], BF16)
        pt = sb("pt", [P, 2, T, N])
        o_sb = sb("o_sb", [P, HG, P])
        r_den = sb("r_den", [P, HG, T])
        attn = sb("attn", [P, T, C])
        attn_t = sb("attn_t", [P, KC, N])
        x_res = sb("x_res", [P, T, C])
        x1 = sb("x1", [P, T, C])
        x_hat2 = sb("x_hat2", [P, T, C])
        x2t = sb("x2t", [P, KC, N])
        y = sb("y", [P, T, C])

        ps_s = ps("ps_s", [P, 2, N])
        ps_t = ps("ps_t", [P, T_BANKS, N])
        ps_o = ps("ps_o", [P, HG, P])
        ps_misc = ps("ps_misc", [P, MiscBanks.BANKS, 512])

        s_ld = sem("s_ld")
        s_ld_tab = sem("s_ld_tab")
        s_w = sem("s_w")
        s_tr = sem("s_tr")
        s_kv = sem("s_kv")
        s_slope = sem("s_slope")
        s_alibi = sem("s_alibi")
        s_rows = sem("s_rows")
        wld = pt[:, 0, :, :].rearrange("p a b -> p (a b)")
        wq_nat = wld[:, 0:6 * C].rearrange("p (a c) -> p a c", a=6)
        wld2 = pt[:, 1, :, :].rearrange("p a b -> p (a b)")
        proj_nat = wld2[:, 0:512].rearrange("p (a c) -> p a c", a=2)
        w_nat = wld2[:, 512:1024].rearrange("p (a c) -> p a c", a=2)
        vr_nat = wld2[:, 1024:1088].rearrange("p (a c) -> p a c", a=2)
        cr_nat = wld2[:, 1088:1152].rearrange("p (a c) -> p a c", a=2)
        toep = y[:, :, :].rearrange("p a b -> p (a b)")
        pat = x1[M_ROW:P, :, :].rearrange("p a b -> p (a b)").rearrange("p (s n) -> p s n", s=2)
        vc_t = x_res[0:R_LORA, 0:2, :].rearrange("p a b -> p (a b)")

        weights = [
            (ident[:, :], consts["ident"]),
            (wq_nat, qkv_w.rearrange("(a p) c -> p a c", p=P)),
            (vr_nat, v_r.rearrange("(a p) c -> p a c", p=P)),
            (cr_nat, c_r.rearrange("(a p) c -> p a c", p=P)),
            (w_nat, w.rearrange("(a p) c -> p a c", p=P)),
            (proj_nat, proj_w.rearrange("(a p) c -> p a c", p=P)),
        ]
        for dst, src in weights:
            sp.dma_start(dst, src).then_inc(s_ld, 16)

        step = [0]

        def chain(engine, instruction):
            instruction.then_inc(s_w, 1)
            step[0] += 1

        dve.memset(v_one[:, :, :, :], 1.0)
        dve.memset(minus_half[:, :], -0.5)
        dve.memset(eps[:, :], EPS)
        dve.memset(ones[:, :], 1.0)
        dve.wait_ge(s_ld, 16 * len(weights))
        dve.tensor_copy(ident_b[:, :], ident[:, :])

        pe.wait_ge(s_ld, 16 * len(weights))
        flat_t = ps_t[:, :, :].rearrange("p a n -> p (a n)")
        flat_o = ps_o[:, :, :].rearrange("p a n -> p (a n)")
        for a in range(2):
            pe.transpose(flat_o[0:R_LORA, a * P:(a + 1) * P], vr_nat[:, a, :], ident[:, :])
        for a in range(2):
            ins = pe.transpose(flat_o[0:R_LORA, C + a * P:C + (a + 1) * P], cr_nat[:, a, :], ident[:, :])
        chain(pe, ins)
        dve.wait_ge(s_w, step[0])
        vc_copy = dve.tensor_copy(vc_t, flat_o[0:R_LORA, :])
        for kc in range(KC):
            for a in range(6):
                pe.transpose(flat_t[:, (kc * 6 + a) * P:(kc * 6 + a + 1) * P],
                             wq_nat[:, a, kc * P:(kc + 1) * P], ident[:, :])
        for kc in range(KC):
            for a in range(2):
                ins = pe.transpose(ps_s[:, kc, a * P:(a + 1) * P], proj_nat[:, a, kc * P:(kc + 1) * P], ident[:, :])
        ins.then_inc(s_tr, 1)
        chain(dve, vc_copy)
        pe.wait_ge(s_w, step[0])
        for kc in range(KC):
            for a in range(2):
                dst = flat_o[:, kc * C + a * P:kc * C + (a + 1) * P]
                pe.matmul(dst, vc_t[:, kc * P:(kc + 1) * P], vc_t[:, C + a * P:C + (a + 1) * P],
                          start=True, stop=False)
                ins = pe.matmul(dst, w_nat[:, a, kc * P:(kc + 1) * P], ident[:, :], start=False, stop=True)
        chain(pe, ins)
        dve.wait_ge(s_tr, 1)
        act.wait_ge(s_tr, 1)
        for kc in range(KC):
            dve.tensor_scalar(wqkv_t[:, kc, 0:C], flat_t[:, kc * 3 * C:kc * 3 * C + C], SCALE, None, ALU.mult)
        dve.tensor_copy(wqkv_t[:, 0, C:3 * C], flat_t[:, C:3 * C])
        dve.tensor_copy(proj_t[:, 0, :], ps_s[:, 0, 0:C])
        act.copy(wqkv_t[:, 1, C:3 * C], flat_t[:, 4 * C:6 * C])
        act.copy(proj_t[:, 1, :], ps_s[:, 1, 0:C]).then_inc(s_kv, 1)
        dve.wait_ge(s_w, step[0])
        chain(dve, dve.tensor_copy(ffn_t[:, :, :].rearrange("p a b -> p (a b)"), flat_o))
        dve.wait_ge(s_w, step[0])
        chain(dve, dve.memset(ps_o[:, :, :], 0.0))
        pe.wait_ge(s_w, step[0])
        pe.wait_ge(s_kv, 1)

        def load_tables(b):
            tables = [
                (slope8[:, :], slopes.partition_broadcast(P)), (pick[:, :], consts["pick"]),
                (rope_cos[:, :], consts["rope_cos"]), (rope_sin[:, :], consts["rope_sin"]),
                (toep[:, 0:U_W], consts["toep"]), (diag[:, :], consts["diag"]),
                (pat, consts["pat"].rearrange("p (s n) -> p s n", s=2)),
                (proj_bias[:, :], proj_b.partition_broadcast(P)),
                (ffn_bias[:, :], wb.partition_broadcast(P)),
            ]
            for dst, src in tables:
                sp.dma_start(dst, src).then_inc(s_ld_tab, 16)
            dve.wait_ge(s_ld_tab, 16 * len(tables))

        slope_steps = [0]

        def slope_parts(b):
            def then(instruction):
                slope_steps[0] += 1
                instruction.then_inc(s_slope, 1)
                dve.wait_ge(s_slope, slope_steps[0])

            then(dve.tensor_scalar(slope8[:, :], slope8[:, :], MAX_BIAS, None, ALU.mult))
            s8 = slope8[M_ROW:P, :]
            then(dve.tensor_copy(partb[:, 0, :], s8))
            then(dve.tensor_tensor(rest[:, 0, :], s8, partb[:, 0, :], ALU.subtract))
            then(dve.tensor_copy(partb[:, 1, :], rest[:, 0, :]))
            then(dve.tensor_tensor(rest[:, 1, :], rest[:, 0, :], partb[:, 1, :], ALU.subtract))
            then(dve.tensor_copy(partb[:, 2, :], rest[:, 1, :]))
            for s in range(2):
                then(dve.tensor_scalar(side[:, s, :], partb[:, 0, :], pick[:, 4 * s:4 * s + 1],
                                       pick[:, 4 * s + 3:4 * s + 4], ALU.mult, ALU.add))
                for i in (1, 2):
                    then(dve.scalar_tensor_tensor(out=side[:, s, :], in0=partb[:, i, :],
                                                  scalar=pick[:, 4 * s + i:4 * s + i + 1], in1=side[:, s, :],
                                                  op0=ALU.mult, op1=ALU.add))
            then(dve.tensor_tensor(side[:, 1, :], side[:, 1, :], pick[:, 8:8 + H], ALU.add))

        def alibi_table(b, h):
            dve.tensor_scalar(alibi[:, h, :], toep[:, 0:U_W], slope8[:, h:h + 1], None, ALU.mult) \
               .then_inc(s_alibi, 1)

        def constant_rows(b, h):
            for s in range(2):
                ins = dve.tensor_scalar(at[M_ROW:P, h, s, :], pat[:, s, :], side[:, s, h:h + 1], None, ALU.mult)
            ins.then_inc(s_rows, 1)

        e_load = event("e_load", 1, 16)
        e_aggr = event("e_aggr", 1)
        e_bn = event("e_bn", 1)
        e_veps = event("e_veps", 1)
        e_rstd = event("e_rstd", 1)
        e_centred = event("e_centred", 1)
        e_xhat = event("e_xhat", 1)
        e_xt = event("e_xt", KC)
        e_rope = event("e_rope", G)
        e_qk = event("e_qk", G)
        e_hi = event("e_hi", G)
        e_r1 = event("e_r1", G)
        e_mid = event("e_mid", G)
        e_lo = event("e_lo", G)
        e_rep = event("e_rep", G)
        e_at = event("e_at", H)
        e_vs = event("e_vs", 2)
        e_v1 = event("e_v1", G)
        e_s = event("e_s", H * T)
        e_mx = event("e_mx", H * T)
        e_mhi = event("e_mhi", G)
        e_m2 = event("e_m2", G)
        e_mt = event("e_mt", G)
        e_mrow = event("e_mrow", G, 16)
        e_st = event("e_st", H * T)
        e_dg = event("e_dg", H * T)
        e_ex = event("e_ex", H * T)
        e_pv = event("e_pv", H)
        e_o = event("e_o", G)
        e_rden = event("e_rden", G)
        e_att = event("e_att", G)
        e_res = event("e_res", 1, 16)
        e_resb = event("e_resb", 1)
        e_aT = event("e_aT", KC)
        e_x1 = event("e_x1", 2)
        e_bn2 = event("e_bn2", 1)
        e_aggr2 = event("e_aggr2", 1)
        e_veps2 = event("e_veps2", 1)
        e_rstd2 = event("e_rstd2", 1)
        e_centred2 = event("e_centred2", 1)
        e_xhat2 = event("e_xhat2", 1)
        e_x1b = event("e_x1b", 1)
        e_x2t = event("e_x2t", KC)
        e_y = event("e_y", 2)
        e_out = event("e_out", 1, 16)
        misc = MiscBanks(sem("misc_full"))

        def load_x(b):
            e_xhat.wait(sp, b.before(), 1)
            sp.dma_start(x_in[:, :, :], x[b.index()].rearrange("(t p) c -> p t c", p=P)) \
              .then_inc(e_load.sem, 16)

        def ln_stats(b, src, ln, bn, aggr, veps, rs):
            for t in range(T):
                ins = dve.bn_stats(stats[:, ln, t, :], src[:, t, :])
            bn.mark(ins)
            bn.wait(dve, b, 1)
            dve.nop(nofuse=True)
            for t in range(T):
                ins = dve.bn_aggr(mean_var[:, ln, t, :], stats[:, ln, t, :])
            aggr.mark(ins)
            aggr.wait(pool, b, 1)
            veps.mark(pool.tensor_tensor(var_eps[:, ln, :], mean_var[:, ln, :, 1], eps[:, :], ALU.add))
            veps.wait(pool, b, 1)
            rs.mark(pool.tensor_tensor(rstd[:, ln, :], var_eps[:, ln, :], minus_half[:, :], ALU.pow))

        def stats1(b):
            e_load.wait(dve, b, 1)
            ln_stats(b, x_in, 0, e_bn, e_aggr, e_veps, e_rstd)

        def normalise(b, src, dst, ln, centred, done):
            def over_channels(column):
                return column.rearrange("p (t o) -> p t o", o=1).broadcast_to([P, T, C])

            (e_rstd2 if ln else e_rstd).wait(pool, b, 1)
            centred.mark(pool.tensor_tensor(dst[:, :, :], src[:, :, :], over_channels(mean_var[:, ln, :, 0]),
                                            ALU.subtract))
            centred.wait(pool, b, 1)
            done.mark(pool.tensor_tensor(dst[:, :, :], dst[:, :, :], over_channels(rstd[:, ln, :]), ALU.mult))

        def transpose_tokens(b, kc, src, dst, ready, ready_n, done):
            bank = ps_misc[:, misc.fill(pe), :]
            ready.wait(pe, b, ready_n)
            for t in range(T):
                ins = pe.transpose(bank[:, t * P:(t + 1) * P], src[:, t, kc * P:(kc + 1) * P], ident[:, :])
            unit = misc.filled(ins, done, b, kc + 1)
            yield
            misc.wait_full(act, b, unit)
            done.mark(act.copy(dst[:, kc, :], bank))

        def project_qk(b, g):
            w0 = HG * D
            bank = ps_misc[:, misc.fill(pe), :]
            if g == 0:
                e_xt.wait(pe, b, KC)
            for t in range(T):
                if t:
                    yield
                for kc in range(KC):
                    wt = wqkv_t[:, kc, 0:2 * C].rearrange("p (s o) -> p s o", s=2)[:, :, g * w0:(g + 1) * w0]
                    dst = bank.rearrange("p (s t o) -> p s t o", s=2, t=T)[:, :, t, :]
                    ins = pe.matmul(dst, xt[:, kc, t * P:(t + 1) * P], wt, start=(kc == 0), stop=(kc == KC - 1))
            unit = misc.filled(ins, e_rope, b, g + 1)
            yield
            misc.wait_full(dve, b, unit)
            prev = (b, g) if g else (b.before(), G)
            e_qk.wait(dve, *prev)
            m2 = bank.rearrange("p (s n) -> p s n", s=2)
            m4 = bank.rearrange("p (s n d) -> p s n d", s=2, d=D)
            b4 = rope_b[:, :, :].rearrange("p s (n d) -> p s n d", d=D)
            s4 = rope_sin[:, :].rearrange("p (o n d) -> p o n d", o=1, d=D)
            cos2 = rope_cos[:, :].rearrange("p (o n) -> p o n", o=1).broadcast_to([P, 2, T * HG * D])
            hd = D // 2
            dve.tensor_tensor(rope_a[:, :, :], m2, cos2, ALU.mult)
            for lo, hi in ((0, hd), (hd, 0)):
                ins = dve.tensor_tensor(b4[:, :, :, lo:lo + hd], m4[:, :, :, hi:hi + hd],
                                        s4[:, :, :, lo:lo + hd].broadcast_to([P, 2, T * HG, hd]), ALU.mult)
            e_rope.mark(ins)
            e_rope.wait(pool, b, g + 1)
            e_qk.mark(pool.tensor_tensor(rope_a[:, :, :], rope_a[:, :, :], rope_b[:, :, :], ALU.add))

        def parts(g):
            return qka[:, g % 2, :, :, :, :, :].rearrange("p s t h e d -> p (s t h) e d")

        a3 = rope_a[:, :, :].rearrange("p s (n d) -> p (s n) d", d=D)
        r3 = rest1[:, :, :].rearrange("p s (n d) -> p (s n) d", d=D)

        def high_parts(b, g):
            q5 = parts(g)
            e_qk.wait(act, b, g + 1)
            e_hi.mark(act.copy(q5[:, :, 0, :], a3))
            e_hi.wait(pool, b, g + 1)
            e_r1.mark(pool.tensor_tensor(r3, a3, q5[:, :, 0, :], ALU.subtract))

        def middle_parts(b, g):
            q5 = parts(g)
            e_r1.wait(act, b, g + 1)
            e_mid.mark(act.copy(q5[:, :, 1, :], r3))
            e_mid.wait(pool, b, g + 1)
            n = T * HG
            pool.tensor_tensor(q5[:, 0:n, 5, :], r3[:, 0:n, :], q5[:, 0:n, 1, :], ALU.subtract)
            e_lo.mark(pool.tensor_tensor(q5[:, n:2 * n, 4, :], r3[:, n:2 * n, :], q5[:, n:2 * n, 1, :],
                                         ALU.subtract))

        def repeat_parts(b, g):
            n, q5 = T * HG, parts(g)
            e_mid.wait(act, b, g + 1)
            act.copy(q5[:, 0:n, 2:5:2, :], q5[:, 0:n, 0:1, :].broadcast_to([P, n, 2, D]))
            act.copy(q5[:, n:2 * n, 3:6:2, :], q5[:, n:2 * n, 0:1, :].broadcast_to([P, n, 2, D]))
            yield
            act.copy(q5[:, 0:n, 3, :], q5[:, 0:n, 1, :])
            e_rep.mark(act.copy(q5[:, n:2 * n, 2, :], q5[:, n:2 * n, 1, :]))

        def operands(b, h):
            g, hh = divmod(h, HG)
            bank = ps_misc[:, misc.fill(pe), :]
            if hh == 0:
                e_lo.wait(pe, b, g + 1)
                e_rep.wait(pe, b, g + 1)
            for s in range(2):
                if s:
                    yield
                for t in range(T):
                    ins = pe.transpose(bank.bitcast(BF16)[0:QK_ROWS, s * N + t * P:s * N + (t + 1) * P],
                                       qka[:, g % 2, s, t, hh, :, :].rearrange("p e d -> p (e d)"), ident_b[:, :])
            unit = misc.filled(ins, e_at, b, h + 1)
            yield
            misc.wait_full(act, b, unit)
            for s in range(2):
                if s:
                    yield
                ins = act.copy(at[0:QK_ROWS, h, s, :], bank.bitcast(BF16)[0:QK_ROWS, s * N:(s + 1) * N])
            e_at.mark(ins)

        def project_v(b, u):
            bank = ps_misc[:, misc.fill(pe), :]
            if u == 0:
                e_xt.wait(pe, b, KC)
            for t in (2 * u, 2 * u + 1):
                for kc in range(KC):
                    if t % 2 or kc:
                        yield
                    ins = pe.matmul(bank[:, (t % 2) * C:(t % 2 + 1) * C], xt[:, kc, t * P:(t + 1) * P],
                                    wqkv_t[:, kc, 2 * C:3 * C], start=(kc == 0), stop=(kc == KC - 1))
            unit = misc.filled(ins, e_vs, b, u + 1)
            yield
            misc.wait_full(act, b, unit)
            e_v1.wait(act, b.before(), G)
            e_vs.mark(act.copy(v_stage[:, 2 * u:2 * u + 2, :].rearrange("p t c -> p (t c)"), bank))

        def place_v(b, g):
            e_vs.wait(pool, b, 2)
            e_pv.wait(pool, b.before(), HG * (g + 1))
            one = ones[:, :].rearrange("p (a b c) -> p a b c", a=1, b=1).broadcast_to([P, T, HG, D])
            e_v1.mark(pool.tensor_tensor(
                v_one[:, :, g * HG:(g + 1) * HG, 0:D],
                v_stage[:, :, g * HG * D:(g + 1) * HG * D].rearrange("p t (h d) -> p t h d", d=D), one, ALU.mult))

        def max_scores(b, h, t):
            if t == 0:
                e_at.wait(pe, b, h + 1)
            k = h * T + t
            e_mx.wait(pe, b, k - 1)
            e_s.mark(pe.matmul(ps_s[:, t % 2, :], at[0:QK_ROWS, h, 0, t * P:(t + 1) * P],
                               at[0:QK_ROWS, h, 1, :], start=True, stop=True))

        def row_maximum(b, h, t):
            k = h * T + t
            g, hh = divmod(h, HG)
            if h % HG == 0 and t == 0:
                e_m2.wait(dve, *((b, g - 1) if g >= 2 else (b.before(), G + g - 1)))
            if b.is_first() and t == 0:
                dve.wait_ge(s_alibi, h + 1)
            e_s.wait(dve, b, k + 1)
            dve.nop(nofuse=True)
            off = (T - 1 - t) * P
            e_mx.mark(dve.tensor_tensor_reduce(junk[:, t, :], ps_s[:, t % 2, :], alibi[:, h, off:off + N], 1.0, LOWEST,
                                               ALU.add, ALU.max, row_max[:, g % 2, t, hh:hh + 1]))

        def split_max(b, g):
            e_mx.wait(pool, b, (g + 1) * HG * T)
            e_mrow.wait(pool, *((b, g) if g else (b.before(), G)))
            one = ones[:, :].rearrange("p (a b) -> p a b", a=1).broadcast_to([P, T, HG])
            e_mhi.mark(pool.tensor_tensor(max2[:, :, :, 0], row_max[:, g % 2, :, :], one, ALU.mult))
            e_mhi.wait(pool, b, g + 1)
            e_m2.mark(pool.tensor_tensor(max2[:, :, :, 1], row_max[:, g % 2, :, :], max2[:, :, :, 0],
                                         ALU.subtract))

        def max_rows(b, g):
            bank = ps_misc[:, misc.fill(pe), :]
            e_m2.wait(pe, b, g + 1)
            for t in range(T):
                ins = pe.transpose(bank.bitcast(BF16)[M_ROW:BIAS_ROW, t * P:(t + 1) * P],
                                   max2[:, t, :, :].rearrange("p h e -> p (h e)"), ident_b[:, :])
            unit = misc.filled(ins, e_mt, b, g + 1)
            yield
            misc.wait_full(act, b, unit)
            if g == 0:
                e_mrow.wait(act, b.before(), G)
            else:
                e_mrow.wait(act, b, g)
            e_mt.mark(act.copy(max_t[M_ROW:BIAS_ROW, :], bank.bitcast(BF16)[M_ROW:BIAS_ROW, 0:N]))
            if b.is_first():
                sp.wait_ge(s_rows, HG * (g + 1))
            e_mt.wait(sp, b, g + 1)
            src = max_t[M_ROW:BIAS_ROW, :].rearrange("p (o n) -> p o n", o=1).broadcast_to([2 * HG, HG, N])
            sp.dma_start(at[M_ROW:BIAS_ROW, g * HG:(g + 1) * HG, 0, :], src).then_inc(e_mrow.sem, 16)

        def exp_scores(b, h, j):
            k = T * h + j
            if h % HG == 0 and j == 0:
                e_mrow.wait(pe, b, h // HG + 1)
            last = k - T_BANKS if k >= T_BANKS else max(n for n in range(H * T) if n % T_BANKS == k)
            e_ex.wait(pe, b if k >= T_BANKS else b.before(), last + 1)
            e_st.mark(pe.matmul(ps_t[:, k % T_BANKS, :], at[:, h, 1, j * P:(j + 1) * P], at[:, h, 0, :],
                                start=True, stop=True))

        def diagonal_bias(b, h, j):
            k = T * h + j
            e_st.wait(dve, b, k + 1)
            block = ps_t[:, k % T_BANKS, j * P:(j + 1) * P]
            e_dg.mark(dve.scalar_tensor_tensor(out=block, in0=diag[:, :], scalar=slope8[:, h:h + 1], in1=block,
                                               op0=ALU.mult, op1=ALU.add))

        def exponentials(b, h, j):
            k = T * h + j
            e_dg.wait(act, b, k + 1)
            if j == 0:
                e_pv.wait(act, b, h - 1)
            e_ex.mark(act.activation(pt[:, h % 2, j, :], ps_t[:, k % T_BANKS, :], ACT.Exp))

        def weighted_values(b, h):
            g, hh = divmod(h, HG)
            if hh == 0:
                e_v1.wait(pe, b, g + 1)
                e_o.wait(pe, *((b, g) if g else (b.before(), G)))
            for j in range(T):
                if j:
                    yield
                e_ex.wait(pe, b, T * h + j + 1)
                for t in range(T):
                    ins = pe.matmul(ps_o[32 * t:32 * t + D + 1, hh, :], v_one[:, j, h, 0:D + 1],
                                    pt[:, h % 2, j, t * P:(t + 1) * P], start=(j == 0), stop=(j == T - 1),
                                    skip_group_check=True)
            e_pv.mark(ins)

        def o_out(b, g):
            e_pv.wait(act, b, HG * (g + 1))
            e_att.wait(act, *((b, g) if g else (b.before(), G)))
            e_o.mark(act.copy(o_sb[:, :, :], ps_o[:, :, :]))

        def attention_out(b, g):
            bank = ps_misc[:, misc.fill(pe), :]
            e_o.wait(pe, b, g + 1)
            for hh in range(HG):
                ins = pe.transpose(bank[:, hh * P:(hh + 1) * P], o_sb[:, hh, :], ident[:, :])
            unit = misc.filled(ins, e_att, b, g + 1)
            yield
            misc.wait_full(dve, b, unit)
            o4 = bank.rearrange("p (h t d) -> p h t d", h=HG, t=T)
            e_rden.mark(dve.reciprocal(r_den[:, :, :], o4[:, :, :, D]))
            e_rden.wait(dve, b, g + 1)
            if g == 0:
                e_aT.wait(dve, b.before(), KC)
            dst = attn[:, :, g * HG * D:(g + 1) * HG * D].rearrange("p t (h d) -> p h t d", d=D)
            den = r_den[:, :, :].rearrange("p h (t o) -> p h t o", o=1).broadcast_to([P, HG, T, D])
            e_att.mark(dve.tensor_tensor(dst, o4[:, :, :, 0:D], den, ALU.mult))

        def load_residual(b):
            e_x1.wait(sp, b.before(), 2)
            sp.dma_start(x_res[:, :, :], x[b.index()].rearrange("(t p) c -> p t c", p=P)) \
              .then_inc(e_res.sem, 16)

        def residual_bias(b):
            e_res.wait(pool, b, 1)
            bias = proj_bias[:, :].rearrange("p (o c) -> p o c", o=1).broadcast_to([P, T, C])
            e_resb.mark(pool.tensor_tensor(x_res[:, :, :], x_res[:, :, :], bias, ALU.add))

        def out_projection(b, u):
            bank = ps_misc[:, misc.fill(pe), :]
            if u == 0:
                e_aT.wait(pe, b, KC)
            for t in (2 * u, 2 * u + 1):
                for kc in range(KC):
                    if t % 2 or kc:
                        yield
                    ins = pe.matmul(bank[:, (t % 2) * C:(t % 2 + 1) * C], attn_t[:, kc, t * P:(t + 1) * P],
                                    proj_t[:, kc, :], start=(kc == 0), stop=(kc == KC - 1))
            unit = misc.filled(ins, e_x1, b, u + 1)
            yield
            misc.wait_full(dve, b, unit)
            if u == 0:
                e_resb.wait(dve, b, 1)
            two = slice(2 * u, 2 * u + 2)
            e_x1.mark(dve.tensor_tensor(x1[:, two, :], bank.rearrange("p (t c) -> p t c", t=2),
                                        x_res[:, two, :], ALU.add))

        def stats2(b):
            e_x1.wait(dve, b, 2)
            ln_stats(b, x1, 1, e_bn2, e_aggr2, e_veps2, e_rstd2)
            e_out.wait(pool, b.before(), 1)
            bias = ffn_bias[:, :].rearrange("p (o c) -> p o c", o=1).broadcast_to([P, T, C])
            e_x1b.mark(pool.tensor_tensor(y[:, :, :], x1[:, :, :], bias, ALU.add))

        def second_linear(b, u):
            bank = ps_misc[:, misc.fill(pe), :]
            if u == 0:
                e_x2t.wait(pe, b, KC)
            for t in (2 * u, 2 * u + 1):
                for kc in range(KC):
                    if t % 2 or kc:
                        yield
                    ins = pe.matmul(bank[:, (t % 2) * C:(t % 2 + 1) * C], x2t[:, kc, t * P:(t + 1) * P],
                                    ffn_t[:, kc, :], start=(kc == 0), stop=(kc == KC - 1))
            unit = misc.filled(ins, e_y, b, u + 1)
            yield
            misc.wait_full(dve, b, unit)
            if u == 0:
                e_x1b.wait(dve, b, 1)
            two = slice(2 * u, 2 * u + 2)
            e_y.mark(dve.tensor_tensor(y[:, two, :], bank.rearrange("p (t c) -> p t c", t=2),
                                       y[:, two, :], ALU.add))

        def store(b):
            e_y.wait(sp, b, 2)
            sp.dma_start(out[b.index()].rearrange("(t p) c -> p t c", p=P), y[:, :, :]).then_inc(e_out.sem, 16)

        pieces = []

        shift = -min(slot for slot, _ in WHEN.values())

        def put(name, later, piece, *args, part=None, to=pieces):
            slot, places = WHEN[name]
            to.append((slot + later + shift, places if part is None else places[part:part + 1], piece, args))

        put("load_x", 0, load_x)
        put("stats1", 0, stats1)
        put("norm1", 0, lambda b: normalise(b, x_in, x_hat, 0, e_centred, e_xhat))
        for kc in range(KC):
            put(f"xt{kc}", 0, lambda b, kc=kc: transpose_tokens(b, kc, x_hat, xt, e_xhat, 1, e_xt))
        for g in range(G):
            put("project_qk", HG * g, project_qk, g)
            put("high", HG * g, high_parts, g)
            put("middle", HG * g, middle_parts, g)
            put("repeat", HG * g, repeat_parts, g)
            put("place_v", HG * g, place_v, g)
            put("split_max", HG * g, split_max, g)
            put("max_rows", HG * g, max_rows, g)
            put("o_out", HG * g, o_out, g)
            put("attention_out", HG * g, attention_out, g)
        for u in range(2):
            put(f"v{u}", 0, project_v, u)
            put("f2" + "ab"[u], 0, out_projection, u)
            put("f4" + "ab"[u], 0, second_linear, u)
        for h in range(H):
            put("operands", h, operands, h)
            put("pv", h, weighted_values, h)
            for t in range(T):
                put("s", h, max_scores, h, t, part=t)
                put("r", h, row_maximum, h, t, part=t)
                put("t", h, exp_scores, h, t, part=t)
                put("d", h, diagonal_bias, h, t, part=t)
                put("e", h, exponentials, h, t, part=t)
        for kc in range(KC):
            put("f1" + "ab"[kc], 0, lambda b, kc=kc: transpose_tokens(b, kc, attn, attn_t, e_att, G, e_aT))
            put("f3" + "ab"[kc], 0, lambda b, kc=kc: transpose_tokens(b, kc, x_hat2, x2t, e_xhat2, 1, e_x2t))
        put("load_residual", 0, load_residual)
        put("residual_bias", 0, residual_bias)
        put("stats2", 0, stats2)
        put("norm2", 0, lambda b: normalise(b, x1, x_hat2, 1, e_centred2, e_xhat2))
        put("store", 0, store)
        assert max(p[0] for p in pieces) < DEPTH * SLOTS and min(p[0] for p in pieces) >= 0

        once = []
        put("load_tables", 0, load_tables, to=once)
        put("slope_parts", 0, slope_parts, to=once)
        for h in range(H):
            put("alibi_table", h // 2, alibi_table, h, to=once)
            put("constant_rows", h, constant_rows, h, to=once)

        def body(i, alive):
            for slot in range(SLOTS):
                now = [p for p in pieces if p[0] % SLOTS == slot and p[0] // SLOTS in alive]
                now += [p for p in once if p[0] == i * SLOTS + slot] if isinstance(i, int) else []
                parts_of = sorted((place, n, k) for n, p in enumerate(now) for k, place in enumerate(p[1]))
                runs = {}
                for _, n, k in parts_of:
                    at_slot, places, piece, args = now[n]
                    if k == 0:
                        runs[n] = piece(Batch(i, at_slot // SLOTS), *args)
                    if runs[n] is not None:
                        done = next(runs[n], "end") == "end"
                        assert done == (k == len(places) - 1), piece

        for i in range(DEPTH):
            body(i, [d for d in range(DEPTH) if 0 <= i - d < NB])

        units = sum(len(p[1]) > 1 for p in pieces if p[2] not in (weighted_values, repeat_parts))
        before, last = misc.n, misc.emptied
        with nc.Fori(DEPTH, NB) as i:
            misc.slope, misc.base, misc.n = units, before - units * DEPTH, 0
            misc.first = before % MiscBanks.BANKS
            misc.emptied = [(ev, Batch(i, b.d + 1), k) for ev, b, k in last]
            body(i, range(DEPTH))
            assert misc.n == units and units % MiscBanks.BANKS == 0
            assert [(ev, b.d, k) for ev, b, k in misc.emptied] == [(ev, b.d, k) for ev, b, k in last]
        misc.first, misc.slope, misc.base, misc.n = 0, 0, 0, before + units * (NB - DEPTH)
        misc.emptied = [(ev, Batch(NB - 1, b.d), k) for ev, b, k in last]
        for i in range(NB, NB + DEPTH - 1):
            body(i, [d for d in range(DEPTH) if 0 <= i - d < NB])
        e_out.wait(sp, Batch(NB - 1, 0), 1)


_INS = ["L0_attn_x", "L0_attn_qkv_w", "L0_attn_proj_w", "L0_attn_proj_b", "L0_attn_slopes",
        "L0_ffn_W", "L0_ffn_b", "L0_ffn_V_r", "L0_ffn_C"]


def kernel(**inputs):
    import numpy as _np
    import concourse.bacc as _bacc
    from concourse import mybir as _mybir
    from concourse.bass_utils import run_bass_kernel_spmd as _run

    nc = _bacc.Bacc("TRN2", target_bir_lowering=False, num_devices=1)
    arrays, args, consts = {}, [], {}
    for name in _INS:
        a = _np.ascontiguousarray(inputs[name])
        arrays[f"in_{name}_dram"] = a
        args.append(nc.dram_tensor(f"in_{name}_dram", a.shape, _mybir.dt.from_np(a.dtype),
                                   kind="ExternalInput").ap())
    for name, a in shape_constants().items():
        a = _np.ascontiguousarray(a)
        arrays[f"const_{name}_dram"] = a
        consts[name] = nc.dram_tensor(f"const_{name}_dram", a.shape, _mybir.dt.from_np(a.dtype),
                                      kind="ExternalInput").ap()
    out = nc.dram_tensor("out_dram", (NB, N, C), _mybir.dt.float32, kind="ExternalOutput").ap()
    layer(nc, *args, consts, out)
    r = _run(nc, [arrays], core_ids=[0])
    return r.results[0]["out_dram"]
```
